# Optimizing a Trainium2 kernel written in Bass

```python
import numpy as np
import jax
import jax.numpy as jnp

def _softmax(x, axis=-1):
    return jax.nn.softmax(x, axis=axis)

def _gelu(x):
    return jax.nn.gelu(x, approximate=True)

def _silu(x):
    return jax.nn.silu(x)

def _sigmoid(x):
    return jax.nn.sigmoid(x)

def _layernorm(x, axis=-1, eps=1e-05):
    m = jnp.mean(x, axis=axis, keepdims=True)
    v = jnp.var(x, axis=axis, keepdims=True)
    return (x - m) / jnp.sqrt(v + eps)

def _scatter_add(tgt, idx, src, axis=0):
    return tgt.at[idx].add(src)

def _segment_sum(src, seg, n):
    return jax.ops.segment_sum(src, seg, n)
kernel_name = 'mk_gnn_preln_d2_gnn_r8_ecd1c1'

def setup_inputs(seed: int=0):
    np.random.seed(seed)
    _w = jnp.asarray

    def _rec_inputs():
        import jax
        import jax.numpy as jnp
        _gk = jax.random.key(seed)
        x = -0.0006008 + 1.001 * jax.random.normal(jax.random.fold_in(_gk, 1), (6250, 128), jnp.float32)
        src = jax.random.randint(jax.random.fold_in(_gk, 2), (100000,), 0, 6250, jnp.int32)
        dst = jnp.minimum((6250 * jax.random.uniform(jax.random.fold_in(_gk, 3), (100000,)) ** 2.0).astype(jnp.int32), 49999)
        _o = jnp.argsort(dst, stable=True)
        src = src[_o]
        dst = dst[_o]
        edge_attr_10 = jax.random.uniform(jax.random.fold_in(_gk, 12), (100000, 10), jnp.float32, 0.0, 1)
        edge_attr_4 = 0.00109026 + 0.999989 * jax.random.normal(jax.random.fold_in(_gk, 13), (100000, 4), jnp.float32)
        edge_type_4 = jax.random.randint(jax.random.fold_in(_gk, 15), (100000,), 0, 4, jnp.int32)
        edge_weight = jax.random.uniform(jax.random.fold_in(_gk, 16), (100000,), jnp.float32, 0.0, 0.999996)
        return (x, src, dst, edge_attr_10, edge_attr_4, edge_type_4, edge_weight)
    x, src, dst, edge_attr_10, edge_attr_4, edge_type_4, edge_weight = _rec_inputs()

    def _L0_gnn_setup():
        import jax, jax.numpy as jnp
        import numpy as np
        NUM_RELATIONS = 4
        N_NODES = 2500
        N_EDGES = 40000
        F_IN = 128
        HID = 128
        EMB = 128

        def _rgcn_conv(x, src, dst, edge_type, edge_weight, W, root, bias):
            xj = x[src]
            m = jnp.zeros((xj.shape[0], W.shape[2]), dtype=x.dtype)
            for r in range(W.shape[0]):
                mask = (edge_type == r).astype(x.dtype)[:, None]
                m = m + mask * (xj @ W[r])
            m = m * edge_weight[:, None]
            out = jax.ops.segment_sum(m, dst, num_segments=x.shape[0])
            return out + x @ root + bias
        key = jax.random.key(seed)
        ks = jax.random.split(key, 10)
        return {'x': jax.random.normal(ks[0], (N_NODES, F_IN), dtype=jnp.float32), 'edge_index': jax.random.randint(ks[1], (2, N_EDGES), 0, N_NODES, dtype=jnp.int64 if jax.config.jax_enable_x64 else jnp.int32).astype(jnp.int32), 'edge_type': jax.random.randint(ks[2], (N_EDGES,), 0, NUM_RELATIONS).astype(jnp.int32), 'edge_weight': jax.random.uniform(ks[3], (N_EDGES,), dtype=jnp.float32), 'W1': jax.random.normal(ks[4], (NUM_RELATIONS, F_IN, HID), dtype=jnp.float32) * 0.05, 'root1': jax.random.normal(ks[5], (F_IN, HID), dtype=jnp.float32) * 0.05, 'b1': jax.random.normal(ks[6], (HID,), dtype=jnp.float32) * 0.05, 'W2': jax.random.normal(ks[7], (NUM_RELATIONS, HID, EMB), dtype=jnp.float32) * 0.05, 'root2': jax.random.normal(ks[8], (HID, EMB), dtype=jnp.float32) * 0.05, 'b2': jax.random.normal(ks[9], (EMB,), dtype=jnp.float32) * 0.05}
    _L0_gnn_all = _L0_gnn_setup()
    _L0_gnn_in = {k: v for k, v in _L0_gnn_all.items() if k in ('W1', 'root1', 'b1', 'W2', 'root2', 'b2')}
    del _L0_gnn_all

    def _L1_gnn_setup():
        import jax, jax.numpy as jnp
        import numpy as np
        N = 6250
        E = 100000
        MUL = 32
        NB = 10
        RN = 100
        NUM_NEIGHBORS = 16
        INV_SQRT3 = 1.0 / np.sqrt(3.0).astype(np.float32)

        def _lin_irreps(x0, x1, W0, W1):
            fan = x0.shape[-1]
            y0 = x0 @ W0 / jnp.sqrt(jnp.asarray(fan, x0.dtype))
            y1 = jnp.einsum('num,uw->nwm', x1, W1) / jnp.sqrt(jnp.asarray(x1.shape[1], x1.dtype))
            return (y0, y1)
        key = jax.random.key(seed)
        ks = jax.random.split(key, 13)
        x = jax.random.normal(ks[0], (N, MUL * 4), jnp.float32)
        edge_src = jax.random.randint(ks[1], (E,), 0, N, dtype=jnp.int32)
        edge_dst = jax.random.randint(ks[2], (E,), 0, N, dtype=jnp.int32)
        edge_attr = jax.random.normal(ks[3], (E, 4), jnp.float32)
        edge_length_embedded = jax.random.uniform(ks[4], (E, NB), dtype=jnp.float32)
        W_si_0e = jax.random.normal(ks[5], (MUL, MUL), jnp.float32)
        W_si_1o = jax.random.normal(ks[6], (MUL, MUL), jnp.float32)
        W_l1_0e = jax.random.normal(ks[7], (MUL, MUL), jnp.float32)
        W_l1_1o = jax.random.normal(ks[8], (MUL, MUL), jnp.float32)
        W_fc1 = jax.random.normal(ks[9], (NB, RN), jnp.float32)
        W_fc2 = jax.random.normal(ks[10], (RN, 4 * MUL), jnp.float32)
        W_l2_0e = jax.random.normal(ks[11], (2 * MUL, MUL), jnp.float32)
        W_l2_1o = jax.random.normal(ks[12], (2 * MUL, MUL), jnp.float32)
        return dict(x=x, edge_src=edge_src, edge_dst=edge_dst, edge_attr=edge_attr, edge_length_embedded=edge_length_embedded, W_si_0e=W_si_0e, W_si_1o=W_si_1o, W_l1_0e=W_l1_0e, W_l1_1o=W_l1_1o, W_fc1=W_fc1, W_fc2=W_fc2, W_l2_0e=W_l2_0e, W_l2_1o=W_l2_1o)
    _L1_gnn_all = _L1_gnn_setup()
    _L1_gnn_in = {k: v for k, v in _L1_gnn_all.items() if k in ('W_si_0e', 'W_si_1o', 'W_l1_0e', 'W_l1_1o', 'W_fc1', 'W_fc2', 'W_l2_0e', 'W_l2_1o')}
    del _L1_gnn_all
    return {'x': x, 'src': src, 'dst': dst, 'edge_attr_10': edge_attr_10, 'edge_attr_4': edge_attr_4, 'edge_type_4': edge_type_4, 'edge_weight': edge_weight, 'L0_gnn_W1': _L0_gnn_in['W1'], 'L0_gnn_root1': _L0_gnn_in['root1'], 'L0_gnn_b1': _L0_gnn_in['b1'], 'L0_gnn_W2': _L0_gnn_in['W2'], 'L0_gnn_root2': _L0_gnn_in['root2'], 'L0_gnn_b2': _L0_gnn_in['b2'], 'L1_gnn_W_si_0e': _L1_gnn_in['W_si_0e'], 'L1_gnn_W_si_1o': _L1_gnn_in['W_si_1o'], 'L1_gnn_W_l1_0e': _L1_gnn_in['W_l1_0e'], 'L1_gnn_W_l1_1o': _L1_gnn_in['W_l1_1o'], 'L1_gnn_W_fc1': _L1_gnn_in['W_fc1'], 'L1_gnn_W_fc2': _L1_gnn_in['W_fc2'], 'L1_gnn_W_l2_0e': _L1_gnn_in['W_l2_0e'], 'L1_gnn_W_l2_1o': _L1_gnn_in['W_l2_1o']}

def reference(x, src, dst, edge_attr_10, edge_attr_4, edge_type_4, edge_weight, L0_gnn_W1, L0_gnn_root1, L0_gnn_b1, L0_gnn_W2, L0_gnn_root2, L0_gnn_b2, L1_gnn_W_si_0e, L1_gnn_W_si_1o, L1_gnn_W_l1_0e, L1_gnn_W_l1_1o, L1_gnn_W_fc1, L1_gnn_W_fc2, L1_gnn_W_l2_0e, L1_gnn_W_l2_1o):
    import jax
    import jax.numpy as jnp

    def _L0_gnn_ref(x, edge_index, edge_type, edge_weight, W1, root1, b1, W2, root2, b2):
        import jax, jax.numpy as jnp
        import numpy as np
        NUM_RELATIONS = 4
        N_NODES = 2500
        N_EDGES = 40000
        F_IN = 128
        HID = 128
        EMB = 128

        def _rgcn_conv(x, src, dst, edge_type, edge_weight, W, root, bias):
            xj = x[src]
            m = jnp.zeros((xj.shape[0], W.shape[2]), dtype=x.dtype)
            for r in range(W.shape[0]):
                mask = (edge_type == r).astype(x.dtype)[:, None]
                m = m + mask * (xj @ W[r])
            m = m * edge_weight[:, None]
            out = jax.ops.segment_sum(m, dst, num_segments=x.shape[0])
            return out + x @ root + bias
        src, dst = (edge_index[0], edge_index[1])
        ew = (edge_weight - edge_weight.min()) / (edge_weight.max() - edge_weight.min() + 1e-08)
        h = jax.nn.relu(_rgcn_conv(x, src, dst, edge_type, ew, W1, root1, b1))
        h = _rgcn_conv(h, src, dst, edge_type, ew, W2, root2, b2)
        return h

    def _L1_gnn_ref(x, edge_src, edge_dst, edge_attr, edge_length_embedded, W_si_0e, W_si_1o, W_l1_0e, W_l1_1o, W_fc1, W_fc2, W_l2_0e, W_l2_1o):
        import jax, jax.numpy as jnp
        import numpy as np
        N = 6250
        E = 100000
        MUL = 32
        NB = 10
        RN = 100
        NUM_NEIGHBORS = 16
        INV_SQRT3 = 1.0 / np.sqrt(3.0).astype(np.float32)

        def _lin_irreps(x0, x1, W0, W1):
            fan = x0.shape[-1]
            y0 = x0 @ W0 / jnp.sqrt(jnp.asarray(fan, x0.dtype))
            y1 = jnp.einsum('num,uw->nwm', x1, W1) / jnp.sqrt(jnp.asarray(x1.shape[1], x1.dtype))
            return (y0, y1)
        n = x.shape[0]
        x0 = x[:, :MUL]
        x1 = x[:, MUL:].reshape(n, MUL, 3)
        h = jax.nn.relu(edge_length_embedded @ W_fc1 / jnp.sqrt(jnp.float32(NB)))
        w = h @ W_fc2 / jnp.sqrt(jnp.float32(RN))
        wA, wB, wC, wD = (w[:, :MUL], w[:, MUL:2 * MUL], w[:, 2 * MUL:3 * MUL], w[:, 3 * MUL:])
        si0, si1 = _lin_irreps(x0, x1, W_si_0e, W_si_1o)
        y0, y1 = _lin_irreps(x0, x1, W_l1_0e, W_l1_1o)
        g0 = y0[edge_src]
        g1 = y1[edge_src]
        sh0 = edge_attr[:, 0]
        sh1 = edge_attr[:, 1:4]
        outA = wA * g0 * sh0[:, None]
        outB = wB[:, :, None] * g0[:, :, None] * sh1[:, None, :]
        outC = wC[:, :, None] * g1 * sh0[:, None, None]
        outD = wD * jnp.einsum('eum,em->eu', g1, sh1) * INV_SQRT3
        seg = lambda v: jax.ops.segment_sum(v, edge_dst, num_segments=n)
        inv_sqrt_nn = 1.0 / jnp.sqrt(jnp.float32(NUM_NEIGHBORS))
        mid0 = jnp.concatenate([seg(outA), seg(outD)], axis=1) * inv_sqrt_nn
        mid1 = jnp.concatenate([seg(outB), seg(outC)], axis=1) * inv_sqrt_nn
        o0, o1 = _lin_irreps(mid0, mid1, W_l2_0e, W_l2_1o)
        out0 = si0 + 0.5 * o0
        out1 = si1 + 0.5 * o1
        return jnp.concatenate([out0, out1.reshape(n, MUL * 3)], axis=1)
    edge_index = jnp.stack([src, dst])
    h = jnp.maximum(_layernorm(x, axis=-1), 0.0)
    x = x + _L0_gnn_ref(h, edge_index, edge_type_4, edge_weight, L0_gnn_W1, L0_gnn_root1, L0_gnn_b1, L0_gnn_W2, L0_gnn_root2, L0_gnn_b2)
    h = jnp.maximum(_layernorm(x, axis=-1), 0.0)
    x = x + _L1_gnn_ref(h, src, dst, edge_attr_4, edge_attr_10, L1_gnn_W_si_0e, L1_gnn_W_si_1o, L1_gnn_W_l1_0e, L1_gnn_W_l1_1o, L1_gnn_W_fc1, L1_gnn_W_fc2, L1_gnn_W_l2_0e, L1_gnn_W_l2_1o)
    return x

_drawn_inputs = setup_inputs


def setup_inputs(seed=0):
    import zlib

    import numpy as np

    out = dict(_drawn_inputs(seed))
    spreads = {}
    factors = {'edge_attr_10': 3.465,
     'L0_gnn_b2': 3.709,
     'L1_gnn_W_l1_1o': 2.852,
     'L1_gnn_W_l2_0e': 3.013}
    for name, (base, spread) in spreads.items():
        noise = np.random.default_rng([zlib.crc32(name.encode()), seed]).standard_normal(out[name].shape)
        drawn = base * np.exp(spread * noise) if base else spread * noise
        out[name] = jnp.asarray(drawn.astype(out[name].dtype))
    for name, factor in factors.items():
        out[name] = (out[name] * factor).astype(out[name].dtype)
    return out
```

```python
from contextlib import ExitStack

import numpy as np

import concourse.bass as bass
from concourse import mybir

P = 128
N = 6250
E = 100000
F = 128
R = 4
MUL = 32
G4 = 4
NBAS = 10
RN = 100
EPS = 1e-5

ST_TILES = 4
ST_EDGES = ST_TILES * P
BODY = 4
BODY_TILES = BODY * ST_TILES
WINDOW = P
NODE_STS = -(-N // P)
FAST_BODIES = -(-(-(-E // ST_EDGES)) // BODY)
GEN_BODIES = -(-(E // ST_EDGES + 1 + NODE_STS) // BODY)
FAST_STS = FAST_BODIES * BODY
GEN_STS = GEN_BODIES * BODY
AHEAD = 4
IN_TILES = (FAST_STS + AHEAD) * ST_TILES
ALL_STS = GEN_STS + AHEAD
ALL_TILES = ALL_STS * ST_TILES
E_TILES = -(-E // P)
NO_NODE = 8191
FAR = 4.0e6

PREP = 4
NODE_BLOCKS = -(-(NODE_STS * P + WINDOW) // (PREP * P)) * PREP
NODES = NODE_BLOCKS * P
PREP_STEPS = NODE_BLOCKS // PREP
OUT_STEPS = (N // P) // PREP
OUT_REST = N - OUT_STEPS * PREP * P

SRC, DST, TYP, EW, SH = 0, 1, 2, 3, 4
FIELDS = 8
ROW = FIELDS + NBAS
ST_P = FAST_STS // 2

def build(nc, d):
    f32, i32 = mybir.dt.float32, mybir.dt.int32
    ALU, ACT, AX = mybir.AluOpType, mybir.ActivationFunctionType, mybir.AxisListType
    IDX = bass.IndirectOffsetOnAxis
    ds = bass.ds

    table_rel = [nc.dram_tensor(f"table_rel{n}", [NODES * R, F], f32).ap() for n in range(2)]
    table_y = nc.dram_tensor("table_y", [NODES, F], f32).ap()
    basis_t = nc.dram_tensor("basis_t", [NBAS, ALL_TILES * P], f32).ap()
    rows_d = nc.dram_tensor("rows_d", [ALL_TILES * P, ROW], f32).ap()
    w0_d = nc.dram_tensor("w0_d", [1, FAST_STS], f32).ap()
    wide_d = nc.dram_tensor("wide_d", [1, FAST_STS], f32).ap()

    ctx = ExitStack()
    with ctx:
        def sb(name, shape, dt=f32):
            return ctx.enter_context(nc.sbuf_tensor(name, shape, dt))

        def sem(name):
            return ctx.enter_context(nc.semaphore(name))

        X = sb("X", [P, NODE_BLOCKS, F])
        ACC = sb("ACC", [P, 2, NODES])
        accf = ACC[:, :, :].rearrange("p h n -> p (h n)")
        rows = [ACC[:, h, :].rearrange("p (b f) -> p b f", f=F) for h in range(2)]
        STAT = sb("STAT", [P, 4, NODE_BLOCKS])
        TB = sb("TB", [P, PREP, R * F])
        V = sb("V", [P, FIELDS, ALL_TILES])
        W0B = sb("W0B", [P, ALL_STS])
        W0I = sb("W0I", [1, ALL_STS + 4], i32)
        NBR = sb("NBR", [1, 1], i32)
        MINMAX = sb("MINMAX", [P, 4])
        MMALL = sb("MMALL", [P, 4])
        WST = sb("WST", [ST_P, 4, 2])
        WIDE = sb("WIDE", [1, FAST_STS + 4])
        WREL = sb("WREL", [F, 2, R * F])
        ROOT = sb("ROOT", [F, 2, F])
        BIAS = sb("BIAS", [F, 2])
        BD = sb("BD", [P, 4, F])
        BDN = sb("BDN", [P, 4, F])
        FC1 = sb("FC1", [NBAS, RN])
        FC2 = sb("FC2", [RN, F])
        IDENT = sb("IDENT", [P, P])
        IOTAI = sb("IOTAI", [P, P], i32)
        IOTA = sb("IOTA", [P, P])
        STAGE = sb("STAGE", [P, BODY, ST_TILES], i32)
        GT = sb("GT", [P, BODY_TILES, F])
        OH = sb("OH", [P, 2, ST_TILES, WINDOW])
        GS = sb("GS", [P, 2, ST_TILES, F])
        MSG = sb("MSG", [P, 2, ST_TILES, 2, F])
        DOT = sb("DOT", [P, ST_TILES, 3, MUL])
        DSUM = sb("DSUM", [P, 2, ST_TILES, MUL])
        WBG = sb("WBG", [P, ST_TILES, MUL])
        EA = sb("EA", [NBAS, BODY, ST_EDGES])
        HR = sb("HR", [RN, 2, ST_EDGES])

        PS = ctx.enter_context(nc.psum_tensor("PS", [P, 8, 512], f32))
        B_OUT, B_HID, B_W, B_TAB = 0, 2, 4, 6

        NS = NODE_STS
        land = accf[:, 0:ALL_TILES * FIELDS].rearrange("p (t f) -> p t f", f=FIELDS)
        at = ALL_TILES * FIELDS

        def carve(n):
            nonlocal at
            at += n
            return accf[:, at - n:at]

        FILL_TILES = ALL_TILES // 16
        FILL = carve(ROW * FILL_TILES).rearrange("p (t f) -> p t f", f=ROW)
        BLK, TMPE = carve(E_TILES), carve(E_TILES)
        ONES, LOWER = carve(P), carve(P)
        SMALL = carve(8 * NS).rearrange("p (k n) -> p k n", n=NS)
        assert at <= 2 * NODES
        DSTS = accf[0:ST_P, 0:2 * ST_EDGES].rearrange("p (k e) -> p k e", k=2)
        DSTM = accf[0:ST_P, 2 * ST_EDGES:4 * ST_EDGES].rearrange("p (k e) -> p k e", k=2)
        BLKI = sb("BLKI", [P, E_TILES], i32)
        SMALLI = sb("SMALLI", [P, NS], i32)
        EROW = sb("EROW", [P, ROW])
        POSI = sb("POSI", [P, 1], i32)
        SLOT = sb("SLOT", [P, ALL_STS])
        SLOTI = sb("SLOTI", [P, ALL_STS], i32)

        s_cstep = sem("const_step")
        s_const = sem("const_ready")
        s_settled = sem("settled")
        s_x = sem("x_loaded")
        s_w = sem("weights_loaded")
        s_bdz = sem("blocks_zeroed")
        s_bd = sem("blocks_loaded")
        s_bdn = sem("block_weights_ready")
        s_dst = sem("supertile_dst_loaded")
        s_edge = sem("edges_loaded")
        s_epad = sem("edge_pads_set")
        s_basis = sem("basis_copied")
        s_v = sem("vector_chain")
        s_wst = sem("spans_measured")
        s_wst_out = sem("spans_stored")
        s_wst_in = sem("spans_back")
        s_nb = sem("bodies_known")
        s_mm = sem("lane_range")
        s_mmall = sem("weight_range")
        s_edges = sem("edge_fields_ready")
        s_xc = sem("centred")
        s_sq = sem("squared")
        s_var = sem("variance")
        s_dev = sem("deviation")
        s_norm = sem("normed")
        g_v = sem("regroup_chain")
        g_fill = sem("fill_ready")
        g_filled = sem("slots_filled")
        g_lane = sem("lane_counts")
        g_tot = sem("block_totals")
        g_tri = sem("regroup_const_step")
        g_const = sem("regroup_const")
        g_hot = sem("block_onehot")
        g_rank = sem("ranks")
        g_row = sem("edge_row_ready")
        g_basis = sem("edge_basis_in")
        g_scat = sem("edge_rows_scattered")
        g_free = sem("edge_row_free")
        g_land = sem("fields_back")
        g_bt = sem("basis_back")
        tp_mm = [sem(f"rows_transposed{n}") for n in range(2)]
        tp_ev = [sem(f"columns_copied{n}") for n in range(2)]
        t_mm = [sem(f"table_product{n}") for n in range(3)]
        t_ev = [[sem(f"table_copied{n}_{k}") for k in range(2)] for n in range(3)]
        t_out = [[sem(f"table_stored{n}_{k}") for k in range(2)] for n in range(3)]
        t_free = [[sem(f"table_slot_free{n}_{k}") for k in range(2)] for n in range(3)]
        r_mm = [sem(f"root_product{n}") for n in range(3)]
        r_ev = [sem(f"root_copied{n}") for n in range(3)]
        staged = [sem(f"indices_staged{n}") for n in range(3)]
        msg_done = [sem(f"messages_summed{n}") for n in range(3)]
        add_done = [sem(f"sums_added{n}") for n in range(3)]
        oh_ready = [sem(f"onehots_ready{n}") for n in range(2)]
        gathered = [sem(f"gathered{j}") for j in range(BODY_TILES)]
        ea = [sem(f"basis_in{j}") for j in range(BODY)]
        fc1_done = sem("fc1_done")
        relu_done = sem("relu_done")
        fc2_done = sem("fc2_done")
        gs_done = sem("scaled_rows_ready")
        prod_done = sem("products_done")
        d_step = sem("product_steps")
        s_relu = sem("layer0_relu")
        x_mm = sem("update_transposed")
        x_ev = sem("update_added")
        f_mm = sem("final_product")
        f_add = sem("final_added")
        s_out = sem("result_stored")

        block = ctx.enter_context(nc.Block())

        HT = [1, 0, 1]
        SUMS = [0, 1]

        def bodies(e):
            e.wait_ge(s_nb, 1)
            return e.value_load(NBR[0:1, 0:1], min_val=FAST_BODIES, max_val=GEN_BODIES)


        def settle(e):
            e.sem_inc(s_settled, 1)

        @block.sync
        def _(sp):
            for n in range(3):
                for k in range(2):
                    sp.sem_inc(t_free[n][k], 1)
            sp.dma_start(X[:, :, :], d["x"].rearrange("(b p) f -> p b f", p=P)).then_inc(s_x, 16)
            for l in range(2):
                sp.dma_start(WREL[:, l, :].rearrange("i (r o) -> i r o", r=R),
                             d[f"W{l + 1}"].rearrange("r i o -> i r o")).then_inc(s_w, 16)
                sp.dma_start(ROOT[:, l, :], d[f"root{l + 1}"]).then_inc(s_w, 16)
                sp.dma_start(BIAS[:, l:l + 1], d[f"b{l + 1}"].rearrange("(f o) -> f o", o=1)).then_inc(s_w, 16)
            sp.dma_start(FC1[:, :], d["fc1"]).then_inc(s_w, 16)
            sp.dma_start(FC2[:, :], d["fc2"]).then_inc(s_w, 16)
            sp.wait_ge(s_wst, 1)
            sp.dma_start(w0_d.rearrange("o (p k) -> (o p) k", k=2), WST[:, 0, :]).then_inc(s_wst_out, 16)
            sp.dma_start(wide_d.rearrange("o (p k) -> (o p) k", k=2), WST[:, 3, :]).then_inc(s_wst_out, 16)
            sp.wait_ge(s_wst_out, 32)
            sp.dma_start(WIDE[:, 0:FAST_STS], wide_d).then_inc(s_wst_in, 16)
            sp.dma_start(W0B[:, 0:FAST_STS], w0_d.to_broadcast([P, FAST_STS])).then_inc(s_wst_in, 16)
            sp.dma_start(basis_t[:, 0:IN_TILES * P], d["basis"]).then_inc(s_basis, 16)
            sp.wait_ge(s_bdz, 1)
            for q in range(G4):
                r = slice(MUL * q, MUL * q + MUL)
                k = min(q, 1)
                sp.dma_start(BD[r, 0, r], d[f"l1_{k}"]).then_inc(s_bd, 16)
                sp.dma_start(BD[r, 1, r], d[f"si{k}"]).then_inc(s_bd, 16)
                sp.dma_start(BD[r, 2, r], d[f"l2_{k}"][0:MUL, :]).then_inc(s_bd, 16)
                sp.dma_start(BD[r, 3, r], d[f"l2_{k}"][MUL:2 * MUL, :]).then_inc(s_bd, 16)
            sp.wait_ge(s_basis, 16)
            nb = bodies(sp)

            with sp.If(nb > FAST_BODIES):
                sp.wait_ge(g_fill, 1)
                fill_v = rows_d.rearrange("(c p t) f -> c p t f", c=16, p=P)
                for c in range(16):
                    sp.dma_start(fill_v[c], FILL).then_inc(g_filled, 16)
                with nc.allow_non_contiguous_dma(reason="edges' basis values, one column each"):
                    with sp.Fori(0, E_TILES) as t:
                        sp.wait_ge(g_free, t + 1)
                        sp.dma_start(EROW[:, FIELDS:ROW],
                                     d["basis"][:, ds(t * P, P)].rearrange("k p -> p k")).then_inc(g_basis, 16)
                sp.wait_ge(g_free, E_TILES + 1)
                sp.dma_start(land, rows_d.rearrange("(t p) f -> p t f", p=P)[:, :, 0:FIELDS]).then_inc(g_land, 16)
                with nc.allow_non_contiguous_dma(reason="basis values, transposed"):
                    with sp.Fori(0, ALL_STS) as s:
                        sp.dma_start(basis_t[:, ds(s * ST_EDGES, ST_EDGES)],
                                     rows_d[ds(s * ST_EDGES, ST_EDGES), FIELDS:ROW].rearrange("e k -> k e")
                                     ).then_inc(g_bt, 16)
                        sp.wait_ge(g_bt, s * 16 + 16)
                        settle(sp)

            def table_out(n, width, dst):
                dst = dst.rearrange("(c p) f -> p c f", p=P)
                with sp.Fori(0, PREP_STEPS) as i:
                    for k in range(2):
                        for e in range(2):
                            sp.wait_ge(t_ev[n][e], i * 2 + k + 2)
                        sp.dma_start(dst[:, ds(i * PREP + 2 * k, 2), :],
                                     TB[:, 2 * k:2 * k + 2, 0:width]).then_inc(t_out[n][k], 16)
                    for k in range(2):
                        sp.wait_ge(t_out[n][k], i * 16 + 16)
                        sp.sem_inc(t_free[n][k], 1)

            for n in range(2):
                table_out(n, R * F, table_rel[n].rearrange("(n r) f -> n (r f)", r=R))
            table_out(2, F, table_y)

            for s in range(BODY):
                sp.dma_start(EA[:, s, :], basis_t[:, s * ST_EDGES:(s + 1) * ST_EDGES]).then_inc(ea[s], 16)
            with sp.Fori(0, nb) as i:
                for s in range(BODY):
                    sp.wait_ge(fc1_done, i * BODY + s + 1)
                    sp.dma_start(EA[:, s, :], basis_t[:, ds((i * BODY + BODY + s) * ST_EDGES, ST_EDGES)]
                                 ).then_inc(ea[s], 16)

            with sp.Fori(0, OUT_STEPS) as i:
                sp.wait_ge(f_add, i + 2)
                sp.dma_start(d["out"][ds(i * PREP * P, PREP * P), :].rearrange("(c p) f -> p c f", p=P),
                             X[:, ds(i * PREP, PREP), :]).then_inc(s_out, 16)
            sp.wait_ge(f_add, OUT_STEPS + 2)
            sp.dma_start(d["out"][OUT_STEPS * PREP * P:N, :], X[0:OUT_REST, OUT_STEPS * PREP, :]).then_inc(s_out, 16)
            sp.wait_ge(s_out, 16 * (OUT_STEPS + 1))
            for s in range(BODY):
                sp.wait_ge(ea[s], nb * 16 + 16)
            settle(sp)

        @block.gpsimd
        def _(pool):
            pool.dma_start(DSTS, d["dst_st"]).then_inc(s_dst, 16)
            nc.gpsimd.memset(V[:, :, IN_TILES:ALL_TILES], 0.0).then_inc(s_epad, 1)
            pool.dma_start(V[:, SRC, 0:IN_TILES], d["src"]).then_inc(s_edge, 16)
            pool.dma_start(V[:, DST, 0:IN_TILES], d["dst"]).then_inc(s_edge, 16)
            pool.dma_start(V[:, TYP, 0:IN_TILES], d["typ"]).then_inc(s_edge, 16)
            pool.dma_start(V[:, EW, 0:IN_TILES], d["ew"]).then_inc(s_edge, 16)
            pool.dma_start(V[:, SH:SH + 4, 0:IN_TILES], d["sh"].rearrange("k p t -> p k t")).then_inc(s_edge, 16)
            nc.gpsimd.memset(BD[:, :, :], 0.0).then_inc(s_bdz, 1)
            nc.gpsimd.iota(IOTAI[:, :], [[1, P]], base=0, channel_multiplier=0).then_inc(s_const, 1)
            nc.gpsimd.memset(IDENT[:, :], 0.0).then_inc(s_cstep, 1)
            pool.wait_ge(s_cstep, 1)
            nc.gpsimd.affine_select(out=IDENT[:, :], in_=IDENT[:, :], compare_op=ALU.not_equal, fill=1.0,
                                    base=0, pattern=[[-1, P]], channel_multiplier=1).then_inc(s_const, 1)
            pool.wait_ge(s_mm, 1)
            nc.gpsimd.partition_all_reduce(MMALL[:, 0:2], MINMAX[:, 0:2], P,
                                           bass.bass_isa.ReduceOp.max).then_inc(s_mmall, 1)
            nb = bodies(pool)

            with pool.If(nb > FAST_BODIES):
                pool.wait_ge(g_lane, 1)
                nc.gpsimd.memset(ONES, 1.0).then_inc(g_tri, 1)
                nc.gpsimd.memset(LOWER, 0.0).then_inc(g_tri, 1)
                nc.gpsimd.iota(SLOTI[:, :], [[ST_EDGES, ALL_STS]], base=0, channel_multiplier=0).then_inc(g_tri, 1)
                pool.wait_ge(g_tri, 3)
                nc.gpsimd.affine_select(out=LOWER, in_=LOWER, compare_op=ALU.is_ge, fill=1.0,
                                        base=0, pattern=[[-1, P]], channel_multiplier=1).then_inc(g_const, 1)
                pool.wait_ge(g_filled, 16 * 16)
                pool.sem_inc(g_free, 1)
                with pool.Fori(0, E_TILES) as t:
                    pool.wait_ge(g_row, t + 1)
                    pool.wait_ge(g_basis, t * 16 + 16)
                    settle(pool)
                    pool.indirect_dma_start(out=rows_d, out_offset=IDX(ap=POSI[:, :], axis=0),
                                            in_=EROW[:, :], in_offset=None,
                                            bounds_check=ALL_TILES * P - 1, oob_is_err=False).then_inc(g_scat, 16)
                    pool.wait_ge(g_scat, t * 16 + 16)
                    pool.sem_inc(g_free, 1)

            def gathers(n, table):
                for k in range(2):
                    pool.wait_ge(t_out[n][k], PREP_STEPS * 16)
                with pool.Fori(0, nb) as i:
                    for s in range(BODY):
                        pool.wait_ge(staged[n], i * BODY + s + 1)
                        settle(pool)
                        for j in range(ST_TILES):
                            pool.indirect_dma_start(out=GT[:, s * ST_TILES + j, :], out_offset=None, in_=table,
                                                    in_offset=IDX(ap=STAGE[:, s, j:j + 1], axis=0)
                                                    ).then_inc(gathered[s * ST_TILES + j], 16)

            for n, table in enumerate([*table_rel, table_y]):
                gathers(n, table)

        @block.vector
        def _(v):
            count = {}

            def link(ins, s=s_v):
                count[s.name] = count.get(s.name, 0) + 1
                ins.then_inc(s, 1)
                v.wait_ge(s, count[s.name])

            for n in range(3):
                v.sem_inc(t_ev[n][1], 1)
                v.sem_inc(add_done[n], 2)
            v.sem_inc(r_ev[2], 1)
            v.sem_inc(x_ev, 1)
            v.sem_inc(prod_done, 2)
            v.sem_inc(f_add, 1)

            v.wait_ge(s_dst, 16)
            nc.vector.tensor_reduce(WST[:, 0, :], DSTS, AX.X, ALU.min)
            link(nc.vector.scalar_tensor_tensor(DSTM, DSTS, float(N), DSTS, ALU.is_lt, ALU.mult))
            link(nc.vector.reduce_max(WST[:, 1, :], DSTM, AX.X))
            link(nc.vector.tensor_tensor(WST[:, 2, :], WST[:, 1, :], WST[:, 0, :], ALU.subtract))
            nc.vector.tensor_scalar(WST[:, 3, :], WST[:, 2, :], float(WINDOW), None, ALU.is_ge).then_inc(s_wst, 1)
            nc.vector.memset(W0B[:, FAST_STS:ALL_STS], 0.0)
            link(nc.vector.memset(W0I[:, :], 0))
            v.wait_ge(s_wst_in, 32)
            link(nc.vector.reduce_max(WIDE[:, FAST_STS:FAST_STS + 1], WIDE[:, 0:FAST_STS], AX.X))
            nc.vector.tensor_scalar(NBR[:, :], WIDE[:, FAST_STS:FAST_STS + 1], float(GEN_BODIES - FAST_BODIES),
                                    float(FAST_BODIES), ALU.mult, ALU.add).then_inc(s_nb, 1)

            v.wait_ge(s_edge, 5 * 16)
            v.wait_ge(s_epad, 1)
            nc.vector.reduce_max(MINMAX[:, 0:1], V[:, EW, 0:E_TILES], AX.X)
            link(nc.vector.tensor_reduce(MINMAX[:, 2:3], V[:, EW, 0:E_TILES], AX.X, ALU.min))
            nc.vector.tensor_scalar(MINMAX[:, 1:2], MINMAX[:, 2:3], -1.0, None, ALU.mult).then_inc(s_mm, 1)
            v.wait_ge(s_const, 2)
            link(nc.vector.tensor_copy(IOTA[:, :], IOTAI[:, :]))

            nb = bodies(v)
            with v.If(nb > FAST_BODIES):
                def glink(ins):
                    link(ins, g_v)

                glink(nc.vector.memset(FILL, 0.0))
                nc.vector.memset(FILL[:, :, DST:DST + 1], float(NO_NODE)).then_inc(g_fill, 1)
                glink(nc.vector.tensor_copy(BLKI[:, :], V[:, DST, 0:E_TILES]))
                glink(nc.vector.tensor_single_scalar(BLKI[:, :], BLKI[:, :], P.bit_length() - 1,
                                                     ALU.arith_shift_right))
                glink(nc.vector.tensor_copy(BLK, BLKI[:, :]))
                done = count[g_v.name]
                with v.Fori(0, NS) as b:
                    nc.vector.tensor_scalar(TMPE, BLK, IOTA[:, ds(b, 1)], None, ALU.is_equal).then_inc(g_v, 1)
                    v.wait_ge(g_v, b * 2 + done + 1)
                    nc.vector.reduce_sum(SMALL[:, 0, ds(b, 1)], TMPE, AX.X).then_inc(g_v, 1)
                    v.wait_ge(g_v, b * 2 + done + 2)
                count[g_v.name] += 2 * NS
                nc.vector.memset(SMALL[:, 1:3, :], 0.0).then_inc(g_lane, 1)
                v.wait_ge(g_tot, 1)
                glink(nc.vector.tensor_scalar(SMALLI[:, :], PS[:, B_OUT, 0:NS], float(ST_EDGES - 1), None, ALU.add))
                shift = ST_EDGES.bit_length() - 1
                glink(nc.vector.tensor_single_scalar(SMALLI[:, :], SMALLI[:, :], shift, ALU.arith_shift_right))
                glink(nc.vector.tensor_single_scalar(SMALLI[:, :], SMALLI[:, :], shift, ALU.arith_shift_left))
                glink(nc.vector.tensor_copy(SMALL[:, 1, 1:NS], SMALLI[:, 0:NS - 1]))
                cur, step = 1, 1
                while step < NS:
                    glink(nc.vector.tensor_copy(SMALL[:, 3 - cur, 0:step], SMALL[:, cur, 0:step]))
                    glink(nc.vector.tensor_tensor(SMALL[:, 3 - cur, step:NS], SMALL[:, cur, step:NS],
                                                  SMALL[:, cur, 0:NS - step], ALU.add))
                    cur, step = 3 - cur, step * 2
                NEXT = SMALL[:, 3, :]
                glink(nc.vector.tensor_copy(NEXT, SMALL[:, cur, :]))
                v.wait_ge(g_const, 1)
                glink(nc.vector.tensor_copy(SLOT[:, :], SLOTI[:, :]))
                glink(nc.vector.memset(W0B[:, :], 0.0))
                done = count[g_v.name]
                with v.Fori(1, NS) as b:
                    nc.vector.scalar_tensor_tensor(W0B[:, :], SLOT[:, :], SMALL[:, cur, ds(b, 1)], W0B[:, :],
                                                   ALU.is_ge, ALU.add).then_inc(g_v, 1)
                    v.wait_ge(g_v, b + done)
                count[g_v.name] += NS - 1
                glink(nc.vector.tensor_scalar(W0B[:, :], W0B[:, :], float(P), None, ALU.mult))
                HOT, AT, ATHOT, POS = (SMALL[:, k, :] for k in range(4, 8))
                done = count[g_v.name]
                with v.Fori(0, E_TILES) as t:
                    nc.vector.tensor_scalar(HOT, IOTA[:, 0:NS], BLK[:, ds(t, 1)], None,
                                            ALU.is_equal).then_inc(g_hot, 1)
                    v.wait_ge(g_free, t + 1)
                    nc.vector.tensor_scalar(POS[:, 1:2], V[:, DST, ds(t, 1)], float(N), FAR,
                                            ALU.is_ge, ALU.mult)
                    v.wait_ge(g_hot, t + 1)
                    v.wait_ge(g_rank, t + 1)
                    nc.vector.tensor_tensor(AT, PS[:, B_OUT, 0:NS], NEXT, ALU.add).then_inc(g_v, 1)
                    v.wait_ge(g_v, t * 4 + done + 1)
                    nc.vector.tensor_tensor(ATHOT, AT, HOT, ALU.mult).then_inc(g_v, 1)
                    v.wait_ge(g_v, t * 4 + done + 2)
                    nc.vector.reduce_sum(POS[:, 0:1], ATHOT, AX.X).then_inc(g_v, 1)
                    nc.vector.tensor_tensor(NEXT, NEXT, PS[:, B_OUT, 64:64 + NS], ALU.add).then_inc(g_v, 1)
                    v.wait_ge(g_v, t * 4 + done + 4)
                    nc.vector.tensor_copy(EROW[:, 0:FIELDS], V[:, :, ds(t, 1)].rearrange("p f o -> p (f o)"))
                    nc.vector.tensor_tensor(POSI[:, :], POS[:, 0:1], POS[:, 1:2], ALU.add).then_inc(g_row, 1)
                count[g_v.name] += 4 * E_TILES
                v.wait_ge(g_land, 16)
                glink(nc.vector.tensor_copy(V[:, :, :].rearrange("p f t -> p t f"), land))

            v.wait_ge(s_mmall, 1)
            dst4 = V[:, DST, :].rearrange("p (s v) -> p s v", v=ST_TILES)
            nc.vector.tensor_tensor(dst4, dst4, W0B[:, :].unsqueeze(2).to_broadcast([P, ALL_STS, ST_TILES]),
                                    ALU.subtract)
            nc.vector.scalar_tensor_tensor(V[:, TYP, :], V[:, SRC, :], float(R), V[:, TYP, :],
                                           ALU.mult, ALU.add)
            nc.vector.tensor_copy(W0I[:, 1:1 + ALL_STS], W0B[0:1, :])
            link(nc.vector.tensor_tensor(MMALL[:, 2:3], MMALL[:, 0:1], MMALL[:, 1:2], ALU.add))
            link(nc.vector.tensor_scalar(MMALL[:, 2:3], MMALL[:, 2:3], 1e-8, None, ALU.add))
            link(nc.vector.reciprocal(MMALL[:, 3:4], MMALL[:, 2:3]))
            nc.vector.tensor_scalar(V[:, EW, :], V[:, EW, :], MMALL[:, 1:2], MMALL[:, 3:4],
                                    ALU.add, ALU.mult).then_inc(s_edges, 1)

            def layer_norm(n):
                stat = [STAT[:, k, :] for k in range(4)]
                wide = [P, NODE_BLOCKS, F]
                link(nc.vector.reduce_sum(stat[0], X[:, :, :], AX.X))
                link(nc.vector.tensor_scalar(stat[1], stat[0], 1.0 / F, None, ALU.mult))
                nc.vector.tensor_tensor(rows[1], X[:, :, :], stat[1].unsqueeze(2).to_broadcast(wide),
                                        ALU.subtract).then_inc(s_xc, 1)
                v.wait_ge(s_sq, n + 1)
                link(nc.vector.reduce_sum(stat[2], rows[0], AX.X))
                nc.vector.tensor_scalar(stat[3], stat[2], 1.0 / F, EPS, ALU.mult, ALU.add).then_inc(s_var, 1)
                v.wait_ge(s_dev, n + 1)
                link(nc.vector.reciprocal(stat[3], stat[0]))
                if n == 0:
                    nc.vector.scalar_tensor_tensor(rows[0], rows[1], 0.0, stat[3].unsqueeze(2).to_broadcast(wide),
                                                   ALU.max, ALU.mult).then_inc(s_norm, 1)
                else:
                    nc.vector.scalar_tensor_tensor(rows[0][:, :, 0:MUL], rows[1][:, :, 0:MUL], 0.0,
                                                   stat[3].unsqueeze(2).to_broadcast([P, NODE_BLOCKS, MUL]),
                                                   ALU.max, ALU.mult)
                    for m in range(3):
                        last = nc.vector.scalar_tensor_tensor(
                            rows[0][:, :, MUL * (m + 1):MUL * (m + 2)],
                            rows[1][:, :, MUL:F].rearrange("p b (u m) -> p b u m", m=3)[:, :, :, m], 0.0,
                            stat[3].unsqueeze(2).to_broadcast([P, NODE_BLOCKS, MUL]), ALU.max, ALU.mult)
                    last.then_inc(s_norm, 1)

            def table_copies(n, width):
                with v.Fori(0, PREP_STEPS) as i:
                    for k in range(2):
                        v.wait_ge(t_mm[n], i * PREP + 2 * k + 2)
                        v.wait_ge(t_free[n][k], i + 1)
                        nc.vector.tensor_copy(TB[:, 2 * k + 1, 0:width], PS[:, B_TAB + 1, 0:width]
                                              ).then_inc(t_ev[n][1], 1)
                    if n == 2:
                        v.wait_ge(r_mm[n], i + 1)
                        x4 = X[:, ds(i * PREP, PREP), :]
                        nc.vector.tensor_tensor(x4, x4, PS[:, B_W, :].rearrange("p (c f) -> p c f", f=F),
                                                ALU.add).then_inc(r_ev[n], 1)

            offs = [v.alloc_register(f"window_{s}") for s in range(BODY)]

            def window_at(s):
                return v.snap(offs[s], min_val=0, max_val=NODES - WINDOW)

            def add_sums(n, half, at, bank, k):
                v.wait_ge(msg_done[n], k + 2)
                v.wait_ge(add_done[n], k + 2)
                acc = ACC[:, half, ds(at, WINDOW)] if n < 2 else ACC[:, :, ds(at, WINDOW)]
                cols = WINDOW if n < 2 else 2 * WINDOW
                sums = PS[:, B_OUT + bank, 0:cols]
                if n == 2:
                    sums = sums.rearrange("p (h w) -> p h w", h=2)
                nc.vector.tensor_tensor(acc, acc, sums, ALU.add).then_inc(add_done[n], 1)

            def rgcn(n):
                link(nc.vector.memset(PS[:, B_OUT + 1, :], 0.0))
                with v.Fori(0, nb) as i:
                    v.load(offs, W0I[0:1, ds(i * BODY, BODY)])
                    at = [window_at(s) for s in range(BODY)]
                    for s in range(BODY):
                        k = i * BODY + s
                        v.wait_ge(msg_done[n], k + 1)
                        for j in range(ST_TILES):
                            t = ds(i * BODY_TILES + s * ST_TILES + j, 1)
                            last = nc.vector.tensor_scalar(OH[:, s % 2, j, :], IOTA[:, :], V[:, DST, t],
                                                           V[:, EW, t], ALU.is_equal, ALU.mult)
                        last.then_inc(oh_ready[n], 1)
                        add_sums(n, SUMS[n], at[s], (s + 1) % 2, k)
                v.load([offs[0]], W0I[0:1, ds(nb * BODY, 1)])
                add_sums(n, SUMS[n], window_at(0), 1, nb * BODY)

            def conv():
                with v.Fori(0, nb) as i:
                    v.load(offs, W0I[0:1, ds(i * BODY, BODY)])
                    at = [window_at(s) for s in range(BODY)]
                    for s in range(BODY):
                        k = i * BODY + s
                        t = ds(i * BODY_TILES + s * ST_TILES, ST_TILES)
                        four = [P, ST_TILES, 3, MUL]
                        g = GT[:, s * ST_TILES:(s + 1) * ST_TILES, :].rearrange("p v (g u) -> p v g u", u=MUL)
                        gs = GS[:, s % 2, :, :].rearrange("p v (g u) -> p v g u", u=MUL)
                        w = PS[:, B_W + s % 2, :].rearrange("p (v g u) -> p v g u", v=ST_TILES, u=MUL)
                        msg = MSG[:, s % 2, :, :, :].rearrange("p v h (g u) -> p v h g u", u=MUL)
                        sh1 = V[:, SH + 1:SH + 4, t].rearrange("p m v -> p v m").unsqueeze(3).to_broadcast(four)
                        v.wait_ge(msg_done[2], k + 1)
                        v.wait_ge(prod_done, k + 2)
                        nc.vector.tensor_tensor(OH[:, s % 2, :, :],
                                                IOTA[:, :].unsqueeze(1).to_broadcast([P, ST_TILES, WINDOW]),
                                                V[:, DST, t].unsqueeze(2).to_broadcast([P, ST_TILES, WINDOW]),
                                                ALU.is_equal)
                        v.wait_ge(gs_done, k + 1)
                        nc.vector.tensor_tensor(DOT[:, :, :, :], g[:, :, 1:4, :], sh1, ALU.mult).then_inc(d_step, 1)
                        v.wait_ge(fc2_done, k + 3)
                        nc.vector.tensor_tensor(WBG[:, :, :], w[:, :, 1, :], g[:, :, 0, :], ALU.mult
                                                ).then_inc(d_step, 1)
                        v.wait_ge(d_step, k * 4 + 1)
                        nc.vector.tensor_tensor(DSUM[:, 0, :, :], DOT[:, :, 0, :], DOT[:, :, 1, :], ALU.add
                                                ).then_inc(d_step, 1)
                        nc.vector.tensor_tensor(msg[:, :, 0, 0, :], w[:, :, 0, :], gs[:, :, 0, :], ALU.mult)
                        v.wait_ge(d_step, k * 4 + 3)
                        nc.vector.tensor_tensor(DSUM[:, 1, :, :], DSUM[:, 0, :, :], DOT[:, :, 2, :], ALU.add
                                                ).then_inc(d_step, 1)
                        nc.vector.tensor_tensor(msg[:, :, 1, 1:4, :], w[:, :, 2, :].unsqueeze(2).to_broadcast(four),
                                                gs[:, :, 1:4, :], ALU.mult)
                        nc.vector.tensor_tensor(msg[:, :, 0, 1:4, :], WBG[:, :, :].unsqueeze(2).to_broadcast(four),
                                                sh1, ALU.mult)
                        v.wait_ge(d_step, k * 4 + 4)
                        nc.vector.tensor_tensor(msg[:, :, 1, 0, :], w[:, :, 3, :], DSUM[:, 1, :, :], ALU.mult
                                                ).then_inc(prod_done, 1)
                        add_sums(2, None, at[s], (s + 1) % 2, k)
                v.load([offs[0]], W0I[0:1, ds(nb * BODY, 1)])
                add_sums(2, None, window_at(0), 1, nb * BODY)

            v.wait_ge(s_x, 16)
            layer_norm(0)
            table_copies(0, R * F)
            v.wait_ge(s_bd, 16 * 16)
            nc.vector.tensor_scalar(BD[:, 0:2, :], BD[:, 0:2, :], float(MUL) ** -0.5, None, ALU.mult)
            link(nc.vector.tensor_scalar(BD[:, 2:4, :], BD[:, 2:4, :],
                                         0.5 * float(2 * MUL) ** -0.5 * 16.0 ** -0.5 * float(RN) ** -0.5,
                                         None, ALU.mult))
            link(nc.vector.tensor_scalar(BD[0:MUL, 3, 0:MUL], BD[0:MUL, 3, 0:MUL], 3.0 ** -0.5, None, ALU.mult))
            nc.vector.tensor_copy(BDN[:, :, 0:MUL], BD[:, :, 0:MUL])
            for m in range(3):
                last = nc.vector.tensor_copy(BDN[:, :, MUL:F].rearrange("p k (u m) -> p k u m", m=3)[:, :, :, m],
                                             BD[:, :, MUL * (m + 1):MUL * (m + 2)])
            last.then_inc(s_bdn, 1)
            v.wait_ge(r_ev[0], PREP_STEPS + 1)
            rgcn(0)
            table_copies(1, R * F)
            v.wait_ge(r_ev[1], PREP_STEPS + 1)
            rgcn(1)
            v.wait_ge(add_done[1], nb * BODY + 3)
            settle(v)
            with v.Fori(0, PREP_STEPS) as i:
                v.wait_ge(x_mm, i + 1)
                x4 = X[:, ds(i * PREP, PREP), :]
                nc.vector.tensor_tensor(x4, x4, PS[:, B_HID, :].rearrange("p (c f) -> p c f", f=F),
                                        ALU.add).then_inc(x_ev, 1)
            v.wait_ge(x_ev, PREP_STEPS + 1)
            layer_norm(1)
            table_copies(2, F)
            v.wait_ge(r_ev[2], PREP_STEPS + 1)
            v.wait_ge(t_mm[2], NODE_BLOCKS)
            nc.vector.memset(PS[:, B_OUT + 1, :], 0.0)
            link(nc.vector.memset(ACC[:, :, :], 0.0))
            conv()
            with v.Fori(0, PREP_STEPS) as i:
                v.wait_ge(f_mm, i + 1)
                x4 = X[:, ds(i * PREP, PREP), :]
                nc.vector.tensor_tensor(x4, x4, PS[:, B_TAB, :].rearrange("p (c f) -> p c f", f=F),
                                        ALU.add).then_inc(f_add, 1)

        @block.scalar
        def _(act):
            for n in range(3):
                act.sem_inc(t_ev[n][0], 1)
            for n in range(2):
                act.sem_inc(tp_ev[n], 1)
                act.sem_inc(r_ev[n], 1)

            def squares_and_roots(n):
                act.wait_ge(s_xc, n + 1)
                nc.scalar.activation(ACC[:, 0, :], ACC[:, 1, :], ACT.Square).then_inc(s_sq, 1)
                act.wait_ge(s_var, n + 1)
                nc.scalar.activation(STAT[:, 0, :], STAT[:, 3, :], ACT.Sqrt).then_inc(s_dev, 1)

            def columns(n):
                with act.Fori(0, PREP_STEPS) as i:
                    act.wait_ge(tp_mm[n], i + 1)
                    nc.scalar.activation(ACC[:, 1, ds(i * PREP * P, PREP * P)], PS[:, B_HID, :],
                                         ACT.Copy).then_inc(tp_ev[n], 1)

            def table_copies(n, width):
                with act.Fori(0, PREP_STEPS) as i:
                    for k in range(2):
                        act.wait_ge(t_mm[n], i * PREP + 2 * k + 1)
                        act.wait_ge(t_free[n][k], i + 1)
                        nc.scalar.activation(TB[:, 2 * k, 0:width], PS[:, B_TAB, 0:width], ACT.Copy
                                             ).then_inc(t_ev[n][0], 1)
                    if n < 2:
                        act.wait_ge(r_mm[n], i + 1)
                        nc.scalar.activation(ACC[:, SUMS[n], ds(i * PREP * P, PREP * P)], PS[:, B_W, :],
                                             ACT.Identity, bias=BIAS[:, n:n + 1]).then_inc(r_ev[n], 1)

            def stage(n, slot, tiles):
                field = TYP if n < 2 else SRC
                nc.scalar.activation(STAGE[:, slot, :], V[:, field, tiles], ACT.Copy).then_inc(staged[n], 1)

            def stage_ahead(n, i, s):
                act.wait_ge(msg_done[n], i * BODY + s + 2)
                stage(n, (s + 3) % BODY, ds(i * BODY_TILES + (s + 3) * ST_TILES, ST_TILES))

            nb = bodies(act)
            squares_and_roots(0)
            columns(0)
            act.wait_ge(s_w, 8 * 16)
            act.wait_ge(s_edges, 1)

            def first_stages(n):
                if n:
                    act.wait_ge(staged[n - 1], nb * BODY + 3)
                for s in range(3):
                    stage(n, s, slice(s * ST_TILES, (s + 1) * ST_TILES))

            for n in range(2):
                first_stages(n)
                table_copies(n, R * F)
                with act.Fori(0, nb) as i:
                    for s in range(BODY):
                        stage_ahead(n, i, s)
                if n == 0:
                    act.wait_ge(add_done[0], nb * BODY + 3)
                    nc.scalar.activation(ACC[:, 0, :], ACC[:, 0, :], ACT.Relu).then_inc(s_relu, 1)
            squares_and_roots(1)
            columns(1)
            first_stages(2)
            table_copies(2, F)

            def relu(slot, k):
                act.wait_ge(fc1_done, k + 1)
                nc.scalar.activation(HR[:, slot, :], PS[0:RN, B_HID + slot, :], ACT.Relu,
                                     scale=float(NBAS) ** -0.5).then_inc(relu_done, 1)

            relu(0, 0)
            with act.Fori(0, nb) as i:
                for s in range(BODY):
                    k = i * BODY + s
                    act.wait_ge(fc2_done, k + 2)
                    relu((s + 1) % 2, k + 1)
                    act.wait_ge(prod_done, k + 1)
                    for j in range(ST_TILES):
                        act.wait_ge(gathered[s * ST_TILES + j], (i + nb * 2 + 1) * 16)
                        last = nc.scalar.activation(GS[:, s % 2, j, :], GT[:, s * ST_TILES + j, :], ACT.Copy,
                                                    scale=V[:, SH, ds(i * BODY_TILES + s * ST_TILES + j, 1)])
                    last.then_inc(gs_done, 1)
                    stage_ahead(2, i, s)

        @block.tensor
        def _(pe):
            for n in range(3):
                pe.sem_inc(msg_done[n], 2)
            pe.sem_inc(fc2_done, 2)
            nb = bodies(pe)

            with pe.If(nb > FAST_BODIES):
                pe.wait_ge(g_const, 1)
                pe.wait_ge(g_lane, 1)
                nc.tensor.matmul(PS[:, B_OUT, 0:NS], ONES, SMALL[:, 0, :], start=True, stop=True).then_inc(g_tot, 1)
                with pe.Fori(0, E_TILES) as t:
                    pe.wait_ge(g_hot, t + 1)
                    nc.tensor.matmul(PS[:, B_OUT, 0:NS], LOWER, SMALL[:, 4, :], start=True, stop=True)
                    nc.tensor.matmul(PS[:, B_OUT, 64:64 + NS], ONES, SMALL[:, 4, :], start=True,
                                     stop=True).then_inc(g_rank, 1)

            def cols(b, n=1):
                return slice(b * P, (b + n) * P)

            def transposes(bank, half, ready, free):
                for i in range(PREP_STEPS):
                    pe.wait_ge(free, i + 1)
                    for c in range(PREP):
                        last = nc.tensor.transpose(PS[:, bank, c * P:(c + 1) * P],
                                                   ACC[:, half, cols(i * PREP + c)], IDENT[:, :])
                    last.then_inc(ready, 1)

            def table_products(n):
                width = R * F if n < 2 else F
                rhs = WREL[:, n, :] if n < 2 else BD[:, 0, :]
                for i in range(PREP_STEPS):
                    for c in range(PREP):
                        pe.wait_ge(t_ev[n][c % 2], i * 2 + c // 2 + 1)
                        nc.tensor.matmul(PS[:, B_TAB + c % 2, 0:width], ACC[:, HT[n], cols(i * PREP + c)],
                                         rhs, start=True, stop=True).then_inc(t_mm[n], 1)
                    pe.wait_ge(r_ev[n], i + 1)
                    if n < 2:
                        nc.tensor.matmul(PS[:, B_W, :], ROOT[:, n, :], ACC[:, HT[n], cols(i * PREP, PREP)],
                                         start=True, stop=True).then_inc(r_mm[n], 1)
                    else:
                        for c in range(PREP):
                            last = nc.tensor.matmul(PS[:, B_W, c * P:(c + 1) * P],
                                                    ACC[:, HT[n], cols(i * PREP + c)], BDN[:, 1, :],
                                                    start=True, stop=True)
                        last.then_inc(r_mm[n], 1)

            pe.wait_ge(s_const, 2)
            pe.wait_ge(s_norm, 1)
            transposes(B_HID, 0, tp_mm[0], tp_ev[0])
            pe.wait_ge(tp_ev[0], PREP_STEPS + 1)
            pe.wait_ge(s_w, 8 * 16)
            for n in range(2):
                if n == 1:
                    pe.wait_ge(s_relu, 1)
                table_products(n)
                with pe.Fori(0, nb) as i:
                    for s in range(BODY):
                        k = i * BODY + s
                        pe.wait_ge(oh_ready[n], k + 1)
                        pe.wait_ge(add_done[n], k + 2)
                        for j in range(ST_TILES):
                            pe.wait_ge(gathered[s * ST_TILES + j], (i + nb * n + 1) * 16)
                            last = nc.tensor.matmul(PS[:, B_OUT + s % 2, 0:WINDOW], GT[:, s * ST_TILES + j, :],
                                                    OH[:, s % 2, j, :], start=j == 0, stop=j == ST_TILES - 1)
                        last.then_inc(msg_done[n], 1)
            pe.wait_ge(add_done[1], nb * BODY + 3)
            transposes(B_HID, 1, x_mm, x_ev)
            pe.wait_ge(s_norm, 2)
            transposes(B_HID, 0, tp_mm[1], tp_ev[1])
            pe.wait_ge(tp_ev[1], PREP_STEPS + 1)
            pe.wait_ge(s_bdn, 1)
            table_products(2)

            def fc1(slot, bank, loads):
                pe.wait_ge(ea[slot], loads * 16)
                nc.tensor.matmul(PS[0:RN, B_HID + bank, :], FC1[:, :], EA[:, slot, :],
                                 start=True, stop=True).then_inc(fc1_done, 1)

            def fc2(slot):
                for j in range(ST_TILES):
                    last = nc.tensor.matmul(PS[:, B_W + slot, j * F:(j + 1) * F], HR[:, slot, j * P:(j + 1) * P],
                                            FC2[:, :], start=True, stop=True)
                last.then_inc(fc2_done, 1)

            fc1(0, 0, 1)
            fc1(1, 1, 1)
            pe.wait_ge(r_ev[2], PREP_STEPS + 1)
            pe.wait_ge(relu_done, 1)
            fc2(0)
            with pe.Fori(0, nb) as i:
                for s in range(BODY):
                    k = i * BODY + s
                    pe.wait_ge(relu_done, k + 1)
                    fc1((s + 2) % BODY, s % 2, i + 1 + (s + 2) // BODY)
                    pe.wait_ge(relu_done, k + 2)
                    pe.wait_ge(prod_done, k + 2)
                    fc2((s + 1) % 2)
                    pe.wait_ge(prod_done, k + 3)
                    pe.wait_ge(add_done[2], k + 2)
                    for h in range(2):
                        for j in range(ST_TILES):
                            last = nc.tensor.matmul(PS[:, B_OUT + s % 2, h * WINDOW:(h + 1) * WINDOW],
                                                    MSG[:, s % 2, j, h, :], OH[:, s % 2, j, :],
                                                    start=j == 0, stop=j == ST_TILES - 1)
                    last.then_inc(msg_done[2], 1)
            pe.wait_ge(add_done[2], nb * BODY + 3)
            for i in range(PREP_STEPS):
                pe.wait_ge(f_add, i + 1)
                for c in range(PREP):
                    for h in range(2):
                        last = nc.tensor.matmul(PS[:, B_TAB, c * F:(c + 1) * F],
                                                ACC[:, h, cols(i * PREP + c)], BDN[:, 2 + h, :],
                                                start=h == 0, stop=h == 1)
                last.then_inc(f_mm, 1)


def kernel(**a):
    import concourse.bacc as bacc
    from concourse.bass_utils import run_bass_kernel_spmd

    a = {k: np.asarray(x) for k, x in a.items()}

    def lanes(x, **pad):
        x = np.pad(x, (0, IN_TILES * P - E), **pad)
        return np.ascontiguousarray(x.reshape(IN_TILES, P).T)

    dst = np.pad(a["dst"], (0, IN_TILES * P - E), constant_values=NO_NODE)
    arrays = {
        "x": np.pad(a["x"], ((0, NODES - N), (0, 0))),
        "src": lanes(a["src"]),
        "dst": np.ascontiguousarray(dst.reshape(IN_TILES, P).T),
        "typ": lanes(a["edge_type_4"]),
        "ew": lanes(a["edge_weight"], mode="edge"),
        "sh": np.stack([lanes(a["edge_attr_4"][:, k]) for k in range(4)]),
        "basis": np.ascontiguousarray(np.pad(a["edge_attr_10"], ((0, IN_TILES * P - E), (0, 0))).T),
        "dst_st": dst[:FAST_STS * ST_EDGES].reshape(ST_P, 2, ST_EDGES),
        "W1": a["L0_gnn_W1"], "root1": a["L0_gnn_root1"], "b1": a["L0_gnn_b1"],
        "W2": a["L0_gnn_W2"], "root2": a["L0_gnn_root2"], "b2": a["L0_gnn_b2"],
        "si0": a["L1_gnn_W_si_0e"], "si1": a["L1_gnn_W_si_1o"],
        "l1_0": a["L1_gnn_W_l1_0e"], "l1_1": a["L1_gnn_W_l1_1o"],
        "fc1": a["L1_gnn_W_fc1"], "fc2": a["L1_gnn_W_fc2"],
        "l2_0": a["L1_gnn_W_l2_0e"], "l2_1": a["L1_gnn_W_l2_1o"],
    }
    nc = bacc.Bacc("TRN2", target_bir_lowering=False, num_devices=1)
    d = {n: nc.dram_tensor(f"in_{n}", x.shape, mybir.dt.from_np(x.dtype), kind="ExternalInput").ap()
         for n, x in arrays.items()}
    d["out"] = nc.dram_tensor("out_x", (N, F), mybir.dt.float32, kind="ExternalOutput").ap()
    build(nc, d)
    r = run_bass_kernel_spmd(nc, [{f"in_{n}": x for n, x in arrays.items()}], core_ids=[0])
    return r.results[0]["out_x"]
```

```python
from contextlib import ExitStack

import numpy as np

import concourse.bass as bass
from concourse import mybir

P = 128
N = 6250
E = 100000
F = 128
R = 4
MUL = 32
G4 = 4
NBAS = 10
RN = 100
EPS = 1e-5

ST_TILES = 4
ST_EDGES = ST_TILES * P
BODY = 4
BODY_TILES = BODY * ST_TILES
WINDOW = P
NODE_STS = -(-N // P)
FAST_BODIES = -(-(-(-E // ST_EDGES)) // BODY)
GEN_BODIES = -(-(E // ST_EDGES + 1 + NODE_STS) // BODY)
FAST_STS = FAST_BODIES * BODY
GEN_STS = GEN_BODIES * BODY
AHEAD = 4
IN_TILES = (FAST_STS + AHEAD) * ST_TILES
ALL_STS = GEN_STS + AHEAD
ALL_TILES = ALL_STS * ST_TILES
E_TILES = -(-E // P)
NO_NODE = 8191
FAR = 4.0e6

PREP = 4
NODE_BLOCKS = -(-(NODE_STS * P + WINDOW) // (PREP * P)) * PREP
NODES = NODE_BLOCKS * P
PREP_STEPS = NODE_BLOCKS // PREP
OUT_STEPS = (N // P) // PREP
X_FIRST = 3 * PREP
OUT_REST = N - OUT_STEPS * PREP * P

SRC, DST, TYP, EW, SH = 0, 1, 2, 3, 4
FIELDS = 8
ROW = FIELDS + NBAS
ST_P = FAST_STS // 2

def build(nc, d):
    f32, i32 = mybir.dt.float32, mybir.dt.int32
    ALU, ACT, AX = mybir.AluOpType, mybir.ActivationFunctionType, mybir.AxisListType
    IDX = bass.IndirectOffsetOnAxis
    ds = bass.ds

    table_rel = [nc.dram_tensor(f"table_rel{n}", [NODES * R, F], f32).ap() for n in range(2)]
    table_y = nc.dram_tensor("table_y", [NODES, F], f32).ap()
    basis_t = nc.dram_tensor("basis_t", [NBAS, ALL_TILES * P], f32).ap()
    rows_d = nc.dram_tensor("rows_d", [ALL_TILES * P, ROW], f32).ap()
    w0_d = nc.dram_tensor("w0_d", [1, FAST_STS], f32).ap()
    wide_d = nc.dram_tensor("wide_d", [1, FAST_STS], f32).ap()

    ctx = ExitStack()
    with ctx:
        def sb(name, shape, dt=f32):
            return ctx.enter_context(nc.sbuf_tensor(name, shape, dt))

        def sem(name):
            return ctx.enter_context(nc.semaphore(name))

        X = sb("X", [P, NODE_BLOCKS, F])
        ACC = sb("ACC", [P, 2, NODES])
        BN = sb("BN", [P, NODE_BLOCKS, 6])
        MOM = sb("MOM", [P, 5, NODE_BLOCKS])
        DEV = sb("DEV", [P, 2, NODE_BLOCKS])
        RDEV = sb("RDEV", [P, NODE_BLOCKS])
        SHIFT = sb("SHIFT", [P, NODE_BLOCKS])
        RW = sb("RW", [P, 2, PREP, F])
        HC = sb("HC", [P, NODES])
        TB = sb("TB", [P, 2, PREP, R * F])
        V = sb("V", [P, FIELDS, ALL_TILES])
        W0B = sb("W0B", [P, ALL_STS])
        W0I = sb("W0I", [1, ALL_STS + 4], i32)
        NBR = sb("NBR", [1, 1], i32)
        MINMAX = sb("MINMAX", [P, 4])
        MMALL = sb("MMALL", [P, 4])
        WST = sb("WST", [ST_P, 4, 2])
        WIDE = sb("WIDE", [1, FAST_STS + 4])
        WREL = sb("WREL", [F, 2, R * F])
        ROOT = sb("ROOT", [F, 2, F])
        BIAS = sb("BIAS", [F, 2])
        BD = sb("BD", [P, 4, F])
        BDN = sb("BDN", [P, 4, F])
        FC1 = sb("FC1", [NBAS, RN])
        FC2 = sb("FC2", [RN, F])
        IDENT = sb("IDENT", [P, P])
        IOTAI = sb("IOTAI", [P, P], i32)
        IOTA = sb("IOTA", [P, P])
        STAGE = sb("STAGE", [P, BODY, ST_TILES], i32)
        GT = sb("GT", [P, BODY_TILES, F])
        OH = sb("OH", [P, 2, ST_TILES, WINDOW])
        GS = sb("GS", [P, 2, ST_TILES, F])
        MSG = TB[:, :, 0:ST_TILES, 0:2 * F].rearrange("p s v (h f) -> p s v h f", f=F)
        DOT = sb("DOT", [P, ST_TILES, 3, MUL])
        DSUM = sb("DSUM", [P, 2, ST_TILES, MUL])
        WBG = sb("WBG", [P, ST_TILES, MUL])
        EA = sb("EA", [NBAS, BODY, ST_EDGES])
        HR = sb("HR", [RN, 2, ST_EDGES])

        PS = ctx.enter_context(nc.psum_tensor("PS", [P, 8, 512], f32))
        B_OUT, B_HID, B_W = 0, 2, 4
        B_TR, B_UP, B_TAB = 1, 2, 4

        NS = NODE_STS
        SOME = 4
        land = ACC[:, 0, 0:ALL_TILES * SOME].rearrange("p (t f) -> p t f", f=SOME)
        at = 0

        def carve(n):
            nonlocal at
            at += n
            return ACC[:, 0, at - n:at]

        FILL_TILES = ALL_TILES // 16
        FILL = carve(ROW * FILL_TILES).rearrange("p (t f) -> p t f", f=ROW)
        BLK, TMPE = carve(E_TILES), carve(E_TILES)
        ONES, LOWER = carve(P), carve(P)
        SMALL = carve(8 * NS).rearrange("p (k n) -> p k n", n=NS)
        assert max(at, ALL_TILES * SOME, 4 * ST_EDGES) <= NODES
        DSTS = ACC[0:ST_P, 0, 0:2 * ST_EDGES].rearrange("p (k e) -> p k e", k=2)
        DSTM = ACC[0:ST_P, 0, 2 * ST_EDGES:4 * ST_EDGES].rearrange("p (k e) -> p k e", k=2)
        at = 0

        def carve_hc(n):
            nonlocal at
            at += n
            return HC[:, at - n:at]

        BLKI, SLOTI = carve_hc(E_TILES).bitcast(i32), carve_hc(ALL_STS).bitcast(i32)
        SLOT, EROW = carve_hc(ALL_STS), carve_hc(ROW)
        SMALLI, POSI = carve_hc(NS).bitcast(i32), carve_hc(1).bitcast(i32)

        s_cstep = sem("const_step")
        s_const = sem("const_ready")
        s_settled = sem("settled")
        s_x = [sem(f"x_loaded{k}") for k in range(2)]
        s_w = sem("weights_loaded")
        s_bdz = sem("blocks_zeroed")
        s_bd = sem("blocks_loaded")
        s_bdn = sem("block_weights_ready")
        s_dst = sem("supertile_dst_loaded")
        s_edge = sem("edges_loaded")
        s_epad = sem("edge_pads_set")
        s_basis = sem("basis_copied")
        s_v = sem("vector_chain")
        s_wst = sem("spans_measured")
        s_wst_out = sem("spans_stored")
        s_wst_in = sem("spans_back")
        s_nb = sem("bodies_known")
        s_mm = sem("lane_range")
        s_mmall = sem("weight_range")
        s_edges = sem("table_rows_ready")
        s_bn = [sem(f"statistics{n}") for n in range(2)]
        s_mom = [sem(f"moments{n}") for n in range(2)]
        s_agg = [sem(f"variances{n}") for n in range(2)]
        s_dev = [sem(f"deviations{n}") for n in range(2)]
        s_rdev = [sem(f"reciprocals{n}") for n in range(2)]
        s_stat = [sem(f"scale_and_shift{n}") for n in range(2)]
        s_norm = [sem(f"rows_normed{n}") for n in range(2)]
        g_v = sem("regroup_chain")
        g_fill = sem("fill_ready")
        g_filled = sem("slots_filled")
        g_lane = sem("lane_counts")
        g_tot = sem("block_totals")
        g_tri = sem("regroup_const_step")
        g_const = sem("regroup_const")
        g_hot = sem("block_onehot")
        g_rank = sem("ranks")
        g_row = sem("edge_row_ready")
        g_basis = sem("edge_basis_in")
        g_scat = sem("edge_rows_scattered")
        g_free = sem("edge_row_free")
        g_land = sem("fields_back")
        g_taken = sem("fields_taken")
        g_bt = sem("basis_back")
        tp_mm = [sem(f"rows_transposed{n}") for n in range(2)]
        ht_ready = [sem(f"columns_ready{n}") for n in range(3)]
        t_mm = [sem(f"table_product{n}") for n in range(3)]
        t_ev = [[sem(f"table_copied{n}_{k}") for k in range(2)] for n in range(3)]
        t_out = [[sem(f"table_stored{n}_{k}") for k in range(2)] for n in range(3)]
        t_free = [sem(f"table_slot_free{n}") for n in range(3)]
        s_zero = [sem(f"sums_zeroed{h}") for h in range(2)]
        r_mm = [sem(f"root_product{n}") for n in range(3)]
        r_ev = [sem(f"root_copied{n}") for n in range(3)]
        staged = [sem(f"indices_staged{n}") for n in range(3)]
        msg_done = [sem(f"messages_summed{n}") for n in range(3)]
        add_done = [sem(f"sums_added{n}") for n in range(3)]
        oh_ready = [sem(f"onehots_ready{n}") for n in range(2)]
        gathered = [sem(f"gathered{j}") for j in range(BODY_TILES)]
        ea = [sem(f"basis_in{j}") for j in range(BODY)]
        fc1_done = sem("fc1_done")
        relu_done = sem("relu_done")
        fc2_done = sem("fc2_done")
        gs_done = sem("scaled_rows_ready")
        prod_done = sem("products_done")
        d_step = sem("product_steps")
        x_mm = sem("update_transposed")
        x_ev = sem("update_added")
        f_mm = sem("final_product")
        f_add = sem("final_added")
        s_out = sem("result_stored")

        block = ctx.enter_context(nc.Block())


        def step_cols(i):
            return ds(i * PREP * P, PREP * P)

        def step_blocks(i):
            return ds(i * PREP, PREP)

        def bodies(e):
            e.wait_ge(s_nb, 1)
            return e.value_load(NBR[0:1, 0:1], min_val=FAST_BODIES, max_val=GEN_BODIES)


        def settle(e):
            e.sem_inc(s_settled, 1)

        @block.sync
        def _(sp):
            for n in range(3):
                sp.sem_inc(t_free[n], 2)
            x_v = d["x"].rearrange("(b p) f -> p b f", p=P)

            def load_x(k, b):
                sp.dma_start(X[:, b, :], x_v[:, b, :]).then_inc(s_x[k], 16)

            load_x(0, slice(0, X_FIRST))
            for l in range(2):
                sp.dma_start(WREL[:, l, :].rearrange("i (r o) -> i r o", r=R),
                             d[f"W{l + 1}"].rearrange("r i o -> i r o")).then_inc(s_w, 16)
                sp.dma_start(ROOT[:, l, :], d[f"root{l + 1}"]).then_inc(s_w, 16)
                sp.dma_start(BIAS[:, l:l + 1], d[f"b{l + 1}"].rearrange("(f o) -> f o", o=1)).then_inc(s_w, 16)
            sp.dma_start(FC1[:, :], d["fc1"]).then_inc(s_w, 16)
            sp.dma_start(FC2[:, :], d["fc2"]).then_inc(s_w, 16)
            load_x(1, slice(X_FIRST, NODE_BLOCKS))
            sp.wait_ge(s_wst, 1)
            sp.dma_start(w0_d.rearrange("o (p k) -> (o p) k", k=2), WST[:, 0, :]).then_inc(s_wst_out, 16)
            sp.dma_start(wide_d.rearrange("o (p k) -> (o p) k", k=2), WST[:, 3, :]).then_inc(s_wst_out, 16)
            sp.wait_ge(s_wst_out, 32)
            sp.dma_start(WIDE[:, 0:FAST_STS], wide_d).then_inc(s_wst_in, 16)
            sp.dma_start(W0B[:, 0:FAST_STS], w0_d.to_broadcast([P, FAST_STS])).then_inc(s_wst_in, 16)
            sp.wait_ge(s_bdz, 1)
            for q in range(G4):
                r = slice(MUL * q, MUL * q + MUL)
                k = min(q, 1)
                rx = r if q == 0 else slice(MUL + q - 1, F, 3)
                sp.dma_start(BD[rx, 0, r], d[f"l1_{k}"]).then_inc(s_bd, 16)
                sp.dma_start(BD[rx, 1, r], d[f"si{k}"]).then_inc(s_bd, 16)
                sp.dma_start(BD[r, 2, r], d[f"l2_{k}"][0:MUL, :]).then_inc(s_bd, 16)
                sp.dma_start(BD[r, 3, r], d[f"l2_{k}"][MUL:2 * MUL, :]).then_inc(s_bd, 16)
            def table_out(n, width, dst):
                dst = dst.rearrange("(c p) f -> p c f", p=P)

                def store(i, parity):
                    for e in range(2):
                        sp.wait_ge(t_ev[n][e], i * 2 + 4)
                    sp.dma_start(dst[:, step_blocks(i), :], TB[:, parity, :, 0:width]).then_inc(t_out[n][parity], 16)

                store(0, 0)
                with sp.Fori(0, PREP_STEPS // 2) as j:
                    for q in range(2):
                        store(j * 2 + 1 + q, 1 - q)
                        sp.wait_ge(t_out[n][q], j * 16 + 16)
                        sp.sem_inc(t_free[n], 1)

            relations = [t.rearrange("(n r) f -> n (r f)", r=R) for t in table_rel]
            table_out(0, R * F, relations[0])
            sp.dma_start(basis_t[:, 0:IN_TILES * P], d["basis"]).then_inc(s_basis, 16)
            sp.wait_ge(s_basis, 16)
            nb = bodies(sp)

            with sp.If(nb > FAST_BODIES):
                sp.wait_ge(g_fill, 1)
                fill_v = rows_d.rearrange("(c p t) f -> c p t f", c=16, p=P)
                for c in range(16):
                    sp.dma_start(fill_v[c], FILL).then_inc(g_filled, 16)
                with nc.allow_non_contiguous_dma(reason="edges' basis values, one column each"):
                    with sp.Fori(0, E_TILES) as t:
                        sp.wait_ge(g_free, t + 1)
                        sp.dma_start(EROW[:, FIELDS:ROW],
                                     d["basis"][:, ds(t * P, P)].rearrange("k p -> p k")).then_inc(g_basis, 16)
                sp.wait_ge(g_free, E_TILES + 1)
                for k in range(FIELDS // SOME):
                    if k:
                        sp.wait_ge(g_taken, k)
                    sp.dma_start(land, rows_d.rearrange("(t p) f -> p t f", p=P)[:, :, k * SOME:(k + 1) * SOME]
                                 ).then_inc(g_land, 16)
                with nc.allow_non_contiguous_dma(reason="basis values, transposed"):
                    with sp.Fori(0, ALL_STS) as s:
                        sp.dma_start(basis_t[:, ds(s * ST_EDGES, ST_EDGES)],
                                     rows_d[ds(s * ST_EDGES, ST_EDGES), FIELDS:ROW].rearrange("e k -> k e")
                                     ).then_inc(g_bt, 16)
                        sp.wait_ge(g_bt, s * 16 + 16)
                        settle(sp)

            table_out(1, R * F, relations[1])
            table_out(2, F, table_y)

            for s in range(BODY):
                sp.dma_start(EA[:, s, :], basis_t[:, s * ST_EDGES:(s + 1) * ST_EDGES]).then_inc(ea[s], 16)
            with sp.Fori(0, nb) as i:
                for s in range(BODY):
                    sp.wait_ge(fc1_done, i * BODY + s + 1)
                    sp.dma_start(EA[:, s, :], basis_t[:, ds((i * BODY + BODY + s) * ST_EDGES, ST_EDGES)]
                                 ).then_inc(ea[s], 16)

            with sp.Fori(0, OUT_STEPS) as i:
                sp.wait_ge(f_add, i + 3)
                sp.dma_start(d["out"][ds(i * PREP * P, PREP * P), :].rearrange("(c p) f -> p c f", p=P),
                             X[:, ds(i * PREP, PREP), :]).then_inc(s_out, 16)
            sp.wait_ge(f_add, OUT_STEPS + 3)
            sp.dma_start(d["out"][OUT_STEPS * PREP * P:N, :], X[0:OUT_REST, OUT_STEPS * PREP, :]).then_inc(s_out, 16)
            sp.wait_ge(s_out, 16 * (OUT_STEPS + 1))
            for s in range(BODY):
                sp.wait_ge(ea[s], nb * 16 + 16)
            settle(sp)

        @block.gpsimd
        def _(pool):
            pool.dma_start(DSTS, d["dst_st"]).then_inc(s_dst, 16)
            pool.dma_start(V[:, SRC, 0:IN_TILES], d["src"]).then_inc(s_edge, 16)
            pool.dma_start(V[:, DST, 0:IN_TILES], d["dst"]).then_inc(s_edge, 16)
            pool.dma_start(V[:, TYP, 0:IN_TILES], d["typ"]).then_inc(s_edge, 16)
            pool.dma_start(V[:, EW, 0:IN_TILES], d["ew"]).then_inc(s_edge, 16)
            pool.dma_start(V[:, SH:SH + 4, 0:IN_TILES], d["sh"].rearrange("k p t -> p k t")).then_inc(s_edge, 16)
            nc.gpsimd.memset(V[:, :, IN_TILES:ALL_TILES], 0.0).then_inc(s_epad, 1)
            nc.gpsimd.memset(BD[:, :, :], 0.0).then_inc(s_bdz, 1)
            nc.gpsimd.iota(IOTAI[:, :], [[1, P]], base=0, channel_multiplier=0).then_inc(s_const, 1)
            nc.gpsimd.memset(IDENT[:, :], 0.0).then_inc(s_cstep, 1)
            pool.wait_ge(s_cstep, 1)
            nc.gpsimd.affine_select(out=IDENT[:, :], in_=IDENT[:, :], compare_op=ALU.not_equal, fill=1.0,
                                    base=0, pattern=[[-1, P]], channel_multiplier=1).then_inc(s_const, 1)
            nc.gpsimd.memset(W0B[:, FAST_STS:ALL_STS], 0.0).then_inc(s_const, 1)
            pool.wait_ge(s_mm, 1)
            nc.gpsimd.partition_all_reduce(MMALL[:, 0:2], MINMAX[:, 0:2], P,
                                           bass.bass_isa.ReduceOp.max).then_inc(s_mmall, 1)
            nb = bodies(pool)

            with pool.If(nb > FAST_BODIES):
                pool.wait_ge(g_lane, 1)
                nc.gpsimd.memset(ONES, 1.0).then_inc(g_tri, 1)
                nc.gpsimd.memset(LOWER, 0.0).then_inc(g_tri, 1)
                nc.gpsimd.iota(SLOTI, [[ST_EDGES, ALL_STS]], base=0, channel_multiplier=0).then_inc(g_tri, 1)
                pool.wait_ge(g_tri, 3)
                nc.gpsimd.affine_select(out=LOWER, in_=LOWER, compare_op=ALU.is_ge, fill=1.0,
                                        base=0, pattern=[[-1, P]], channel_multiplier=1).then_inc(g_const, 1)
                pool.wait_ge(g_filled, 16 * 16)
                pool.sem_inc(g_free, 1)
                with pool.Fori(0, E_TILES) as t:
                    pool.wait_ge(g_row, t + 1)
                    pool.wait_ge(g_basis, t * 16 + 16)
                    settle(pool)
                    pool.indirect_dma_start(out=rows_d, out_offset=IDX(ap=POSI, axis=0),
                                            in_=EROW, in_offset=None,
                                            bounds_check=ALL_TILES * P - 1, oob_is_err=False).then_inc(g_scat, 16)
                    pool.wait_ge(g_scat, t * 16 + 16)
                    pool.sem_inc(g_free, 1)

            def gathers(n, table):
                for k in range(2):
                    pool.wait_ge(t_out[n][k], (PREP_STEPS + 1 - k) // 2 * 16)
                with pool.Fori(0, nb) as i:
                    for s in range(BODY):
                        pool.wait_ge(staged[n], i * BODY + s + 1)
                        settle(pool)
                        for j in range(ST_TILES):
                            pool.indirect_dma_start(out=GT[:, s * ST_TILES + j, :], out_offset=None, in_=table,
                                                    in_offset=IDX(ap=STAGE[:, s, j:j + 1], axis=0)
                                                    ).then_inc(gathered[s * ST_TILES + j], 16)

            gathers(0, table_rel[0])
            gathers(1, table_rel[1])
            pool.wait_ge(t_mm[1], NODE_BLOCKS)
            pool.wait_ge(r_mm[1], PREP_STEPS)
            nc.gpsimd.memset(ACC[:, 0, :], 0.0).then_inc(s_zero[0], 1)
            pool.wait_ge(x_mm, PREP_STEPS)
            nc.gpsimd.memset(ACC[:, 1, :], 0.0).then_inc(s_zero[1], 1)
            gathers(2, table_y)

        @block.vector
        def _(v):
            count = {}

            def link(ins, s=s_v):
                count[s.name] = count.get(s.name, 0) + 1
                ins.then_inc(s, 1)
                v.wait_ge(s, count[s.name])

            def statistics(n, i):
                for c in range(PREP):
                    b = ds(i * PREP + c, 1)
                    last = nc.vector.bn_stats(BN[:, b, :].rearrange("p o k -> p (o k)"),
                                              X[:, b, :].rearrange("p o f -> p (o f)"))
                last.then_inc(s_bn[n], 1)
                v.wait_ge(s_bn[n], i + 1)
                b = step_blocks(i)
                even, odd = BN[:, b, 1], BN[:, b, 4]
                nc.vector.tensor_tensor(MOM[:, 1, b], even, odd, ALU.subtract)
                nc.vector.tensor_tensor(MOM[:, 2, b], BN[:, b, 2], BN[:, b, 5], ALU.add).then_inc(s_mom[n], 1)
                nc.vector.tensor_tensor(MOM[:, 0, b], even, odd, ALU.add)
                v.wait_ge(s_mom[n], i * 2 + 1)
                nc.vector.tensor_scalar(MOM[:, 3, b], MOM[:, 2, b], 1.0 / F, EPS, ALU.mult, ALU.add)
                nc.vector.scalar_tensor_tensor(MOM[:, 4, b], MOM[:, 1, b], 0.25, MOM[:, 1, b],
                                               ALU.mult, ALU.mult).then_inc(s_mom[n], 1)
                v.wait_ge(s_mom[n], i * 2 + 2)
                nc.vector.tensor_tensor(DEV[:, 0, b], MOM[:, 4, b], MOM[:, 3, b], ALU.add).then_inc(s_agg[n], 1)

            def scale_and_shift(n, i):
                b = step_blocks(i)
                v.wait_ge(s_dev[n], i + 1)
                nc.vector.reciprocal(RDEV[:, b], DEV[:, 1, b]).then_inc(s_rdev[n], 1)
                v.wait_ge(s_rdev[n], i + 1)
                nc.vector.scalar_tensor_tensor(SHIFT[:, b], MOM[:, 0, b], -0.5, RDEV[:, b],
                                               ALU.mult, ALU.mult).then_inc(s_stat[n], 1)

            def table_copies(n, width, i):
                for c in (1, 3):
                    v.wait_ge(t_mm[n], i * PREP + c + 1)
                    v.wait_ge(t_free[n], i + 1)
                    nc.vector.tensor_copy(TB[:, ds(i % 2, 1), c, 0:width].rearrange("p o f -> p (o f)"),
                                          PS[:, B_TAB + c, 0:width]).then_inc(t_ev[n][1], 1)

            def root_copies(n):
                with v.Fori(0, PREP_STEPS) as i:
                    v.wait_ge(r_mm[n], i + 1)
                    r = PS[:, ds(B_TAB + i % 4, 1), :]
                    if n < 2:
                        nc.vector.tensor_scalar(ACC[:, n, step_cols(i)], r.rearrange("p o n -> p (o n)"),
                                                BIAS[:, n:n + 1], None, ALU.add).then_inc(r_ev[n], 1)
                    else:
                        x4 = X[:, step_blocks(i), :]
                        nc.vector.tensor_tensor(x4, x4, r.rearrange("p o (c f) -> p (o c) f", f=F),
                                                ALU.add).then_inc(r_ev[n], 1)
                v.wait_ge(r_ev[n], PREP_STEPS + 4)

            for n in range(3):
                v.sem_inc(t_ev[n][1], 2)
                v.sem_inc(add_done[n], 2)
                v.sem_inc(r_ev[n], 4)
            v.sem_inc(x_ev, 1)
            v.sem_inc(prod_done, 2)
            v.sem_inc(f_add, 2)

            v.wait_ge(s_x[0], 16)
            for i in range(2):
                statistics(0, i)
                scale_and_shift(0, i)
            v.wait_ge(s_dst, 16)
            nc.vector.tensor_reduce(WST[:, 0, :], DSTS, AX.X, ALU.min)
            link(nc.vector.scalar_tensor_tensor(DSTM, DSTS, float(N), DSTS, ALU.is_lt, ALU.mult))
            link(nc.vector.reduce_max(WST[:, 1, :], DSTM, AX.X))
            link(nc.vector.tensor_tensor(WST[:, 2, :], WST[:, 1, :], WST[:, 0, :], ALU.subtract))
            nc.vector.tensor_scalar(WST[:, 3, :], WST[:, 2, :], float(WINDOW), None, ALU.is_ge).then_inc(s_wst, 1)
            link(nc.vector.memset(W0I[:, :], 0))

            def table_step(i):
                statistics(0, i + 2)
                scale_and_shift(0, i + 2)
                table_copies(0, R * F, i)

            v.wait_ge(s_x[1], 16)
            table_step(0)
            v.wait_ge(s_edge, 5 * 16)
            nc.vector.reduce_max(MINMAX[:, 0:1], V[:, EW, 0:E_TILES], AX.X)
            link(nc.vector.tensor_reduce(MINMAX[:, 2:3], V[:, EW, 0:E_TILES], AX.X, ALU.min))
            nc.vector.tensor_scalar(MINMAX[:, 1:2], MINMAX[:, 2:3], -1.0, None, ALU.mult).then_inc(s_mm, 1)
            v.wait_ge(s_const, 3)
            link(nc.vector.tensor_copy(IOTA[:, :], IOTAI[:, :]))
            v.wait_ge(s_wst_in, 32)
            link(nc.vector.reduce_max(WIDE[:, FAST_STS:FAST_STS + 1], WIDE[:, 0:FAST_STS], AX.X))
            nc.vector.tensor_scalar(NBR[:, :], WIDE[:, FAST_STS:FAST_STS + 1], float(GEN_BODIES - FAST_BODIES),
                                    float(FAST_BODIES), ALU.mult, ALU.add).then_inc(s_nb, 1)

            with v.Fori(1, PREP_STEPS - 2) as i:
                table_step(i)
            for i in (PREP_STEPS - 2, PREP_STEPS - 1):
                table_copies(0, R * F, i)

            nb = bodies(v)
            with v.If(nb > FAST_BODIES):
                def glink(ins):
                    link(ins, g_v)

                glink(nc.vector.memset(FILL, 0.0))
                nc.vector.memset(FILL[:, :, DST:DST + 1], float(NO_NODE)).then_inc(g_fill, 1)
                glink(nc.vector.tensor_copy(BLKI, V[:, DST, 0:E_TILES]))
                glink(nc.vector.tensor_single_scalar(BLKI, BLKI, P.bit_length() - 1,
                                                     ALU.arith_shift_right))
                glink(nc.vector.tensor_copy(BLK, BLKI))
                done = count[g_v.name]
                with v.Fori(0, NS) as b:
                    nc.vector.tensor_scalar(TMPE, BLK, IOTA[:, ds(b, 1)], None, ALU.is_equal).then_inc(g_v, 1)
                    v.wait_ge(g_v, b * 2 + done + 1)
                    nc.vector.reduce_sum(SMALL[:, 0, ds(b, 1)], TMPE, AX.X).then_inc(g_v, 1)
                    v.wait_ge(g_v, b * 2 + done + 2)
                count[g_v.name] += 2 * NS
                nc.vector.memset(SMALL[:, 1:3, :], 0.0).then_inc(g_lane, 1)
                v.wait_ge(g_tot, 1)
                glink(nc.vector.tensor_scalar(SMALLI, PS[:, B_OUT, 0:NS], float(ST_EDGES - 1), None, ALU.add))
                shift = ST_EDGES.bit_length() - 1
                glink(nc.vector.tensor_single_scalar(SMALLI, SMALLI, shift, ALU.arith_shift_right))
                glink(nc.vector.tensor_single_scalar(SMALLI, SMALLI, shift, ALU.arith_shift_left))
                glink(nc.vector.tensor_copy(SMALL[:, 1, 1:NS], SMALLI[:, 0:NS - 1]))
                cur, step = 1, 1
                while step < NS:
                    glink(nc.vector.tensor_copy(SMALL[:, 3 - cur, 0:step], SMALL[:, cur, 0:step]))
                    glink(nc.vector.tensor_tensor(SMALL[:, 3 - cur, step:NS], SMALL[:, cur, step:NS],
                                                  SMALL[:, cur, 0:NS - step], ALU.add))
                    cur, step = 3 - cur, step * 2
                NEXT = SMALL[:, 3, :]
                glink(nc.vector.tensor_copy(NEXT, SMALL[:, cur, :]))
                v.wait_ge(g_const, 1)
                glink(nc.vector.tensor_copy(SLOT, SLOTI))
                glink(nc.vector.memset(W0B[:, :], 0.0))
                done = count[g_v.name]
                with v.Fori(1, NS) as b:
                    nc.vector.scalar_tensor_tensor(W0B[:, :], SLOT, SMALL[:, cur, ds(b, 1)], W0B[:, :],
                                                   ALU.is_ge, ALU.add).then_inc(g_v, 1)
                    v.wait_ge(g_v, b + done)
                count[g_v.name] += NS - 1
                glink(nc.vector.tensor_scalar(W0B[:, :], W0B[:, :], float(P), None, ALU.mult))
                HOT, AT, ATHOT, POS = (SMALL[:, k, :] for k in range(4, 8))
                done = count[g_v.name]
                with v.Fori(0, E_TILES) as t:
                    nc.vector.tensor_scalar(HOT, IOTA[:, 0:NS], BLK[:, ds(t, 1)], None,
                                            ALU.is_equal).then_inc(g_hot, 1)
                    v.wait_ge(g_free, t + 1)
                    nc.vector.tensor_scalar(POS[:, 1:2], V[:, DST, ds(t, 1)], float(N), FAR,
                                            ALU.is_ge, ALU.mult)
                    v.wait_ge(g_hot, t + 1)
                    v.wait_ge(g_rank, t + 1)
                    nc.vector.tensor_tensor(AT, PS[:, B_OUT, 0:NS], NEXT, ALU.add).then_inc(g_v, 1)
                    v.wait_ge(g_v, t * 4 + done + 1)
                    nc.vector.tensor_tensor(ATHOT, AT, HOT, ALU.mult).then_inc(g_v, 1)
                    v.wait_ge(g_v, t * 4 + done + 2)
                    nc.vector.reduce_sum(POS[:, 0:1], ATHOT, AX.X).then_inc(g_v, 1)
                    nc.vector.tensor_tensor(NEXT, NEXT, PS[:, B_OUT, 64:64 + NS], ALU.add).then_inc(g_v, 1)
                    v.wait_ge(g_v, t * 4 + done + 4)
                    nc.vector.tensor_copy(EROW[:, 0:FIELDS], V[:, :, ds(t, 1)].rearrange("p f o -> p (f o)"))
                    nc.vector.tensor_tensor(POSI, POS[:, 0:1], POS[:, 1:2], ALU.add).then_inc(g_row, 1)
                count[g_v.name] += 4 * E_TILES
                for k in range(FIELDS // SOME):
                    v.wait_ge(g_land, 16 * k + 16)
                    nc.vector.tensor_copy(V[:, k * SOME:(k + 1) * SOME, :].rearrange("p f t -> p t f"), land
                                          ).then_inc(g_taken, 1)
                v.wait_ge(g_taken, FIELDS // SOME)

            v.wait_ge(s_const, 3)
            nc.vector.scalar_tensor_tensor(V[:, TYP, :], V[:, SRC, :], float(R), V[:, TYP, :],
                                           ALU.mult, ALU.add).then_inc(s_edges, 1)
            dst4 = V[:, DST, :].rearrange("p (s v) -> p s v", v=ST_TILES)
            nc.vector.tensor_tensor(dst4, dst4, W0B[:, :].unsqueeze(2).to_broadcast([P, ALL_STS, ST_TILES]),
                                    ALU.subtract)
            nc.vector.tensor_copy(W0I[:, 1:1 + ALL_STS], W0B[0:1, :])
            v.wait_ge(s_mmall, 1)
            link(nc.vector.tensor_tensor(MMALL[:, 2:3], MMALL[:, 0:1], MMALL[:, 1:2], ALU.add))
            link(nc.vector.tensor_scalar(MMALL[:, 2:3], MMALL[:, 2:3], 1e-8, None, ALU.add))
            link(nc.vector.reciprocal(MMALL[:, 3:4], MMALL[:, 2:3]))
            link(nc.vector.tensor_scalar(V[:, EW, :], V[:, EW, :], MMALL[:, 1:2], MMALL[:, 3:4],
                                         ALU.add, ALU.mult))

            offs = [v.alloc_register(f"window_{s}") for s in range(BODY)]

            def window_at(s):
                return v.snap(offs[s], min_val=0, max_val=NODES - WINDOW)

            def add_sums(n, half, at, bank, k):
                v.wait_ge(msg_done[n], k + 2)
                v.wait_ge(add_done[n], k + 2)
                acc = ACC[:, half, ds(at, WINDOW)] if n < 2 else ACC[:, :, ds(at, WINDOW)]
                cols = WINDOW if n < 2 else 2 * WINDOW
                sums = PS[:, B_OUT + bank, 0:cols]
                if n == 2:
                    sums = sums.rearrange("p (h w) -> p h w", h=2)
                nc.vector.tensor_tensor(acc, acc, sums, ALU.add).then_inc(add_done[n], 1)

            def rgcn(n):
                link(nc.vector.memset(PS[:, B_OUT + 1, :], 0.0))
                with v.Fori(0, nb) as i:
                    v.load(offs, W0I[0:1, ds(i * BODY, BODY)])
                    at = [window_at(s) for s in range(BODY)]
                    for s in range(BODY):
                        k = i * BODY + s
                        v.wait_ge(msg_done[n], k + 1)
                        for j in range(ST_TILES):
                            t = ds(i * BODY_TILES + s * ST_TILES + j, 1)
                            last = nc.vector.tensor_scalar(OH[:, s % 2, j, :], IOTA[:, :], V[:, DST, t],
                                                           V[:, EW, t], ALU.is_equal, ALU.mult)
                        last.then_inc(oh_ready[n], 1)
                        add_sums(n, n, at[s], (s + 1) % 2, k)
                v.load([offs[0]], W0I[0:1, ds(nb * BODY, 1)])
                add_sums(n, n, window_at(0), 1, nb * BODY)

            def conv():
                with v.Fori(0, nb) as i:
                    v.load(offs, W0I[0:1, ds(i * BODY, BODY)])
                    at = [window_at(s) for s in range(BODY)]
                    for s in range(BODY):
                        k = i * BODY + s
                        t = ds(i * BODY_TILES + s * ST_TILES, ST_TILES)
                        four = [P, ST_TILES, 3, MUL]
                        g = GT[:, s * ST_TILES:(s + 1) * ST_TILES, :].rearrange("p v (g u) -> p v g u", u=MUL)
                        gs = GS[:, s % 2, :, :].rearrange("p v (g u) -> p v g u", u=MUL)
                        w = PS[:, B_W + s % 2, :].rearrange("p (v g u) -> p v g u", v=ST_TILES, u=MUL)
                        msg = MSG[:, s % 2].rearrange("p v h (g u) -> p v h g u", u=MUL)
                        sh1 = V[:, SH + 1:SH + 4, t].rearrange("p m v -> p v m").unsqueeze(3).to_broadcast(four)
                        v.wait_ge(msg_done[2], k + 1)
                        v.wait_ge(prod_done, k + 2)
                        nc.vector.tensor_tensor(OH[:, s % 2, :, :],
                                                IOTA[:, :].unsqueeze(1).to_broadcast([P, ST_TILES, WINDOW]),
                                                V[:, DST, t].unsqueeze(2).to_broadcast([P, ST_TILES, WINDOW]),
                                                ALU.is_equal)
                        v.wait_ge(gs_done, k + 1)
                        nc.vector.tensor_tensor(DOT[:, :, :, :], g[:, :, 1:4, :], sh1, ALU.mult).then_inc(d_step, 1)
                        v.wait_ge(fc2_done, k + 3)
                        nc.vector.tensor_tensor(WBG[:, :, :], w[:, :, 1, :], g[:, :, 0, :], ALU.mult
                                                ).then_inc(d_step, 1)
                        v.wait_ge(d_step, k * 4 + 1)
                        nc.vector.tensor_tensor(DSUM[:, 0, :, :], DOT[:, :, 0, :], DOT[:, :, 1, :], ALU.add
                                                ).then_inc(d_step, 1)
                        nc.vector.tensor_tensor(msg[:, :, 0, 0, :], w[:, :, 0, :], gs[:, :, 0, :], ALU.mult)
                        v.wait_ge(d_step, k * 4 + 3)
                        nc.vector.tensor_tensor(DSUM[:, 1, :, :], DSUM[:, 0, :, :], DOT[:, :, 2, :], ALU.add
                                                ).then_inc(d_step, 1)
                        nc.vector.tensor_tensor(msg[:, :, 1, 1:4, :], w[:, :, 2, :].unsqueeze(2).to_broadcast(four),
                                                gs[:, :, 1:4, :], ALU.mult)
                        nc.vector.tensor_tensor(msg[:, :, 0, 1:4, :], WBG[:, :, :].unsqueeze(2).to_broadcast(four),
                                                sh1, ALU.mult)
                        v.wait_ge(d_step, k * 4 + 4)
                        nc.vector.tensor_tensor(msg[:, :, 1, 0, :], w[:, :, 3, :], DSUM[:, 1, :, :], ALU.mult
                                                ).then_inc(prod_done, 1)
                        add_sums(2, None, at[s], (s + 1) % 2, k)
                v.load([offs[0]], W0I[0:1, ds(nb * BODY, 1)])
                add_sums(2, None, window_at(0), 1, nb * BODY)

            v.wait_ge(s_w, 8 * 16)
            root_copies(0)
            v.wait_ge(s_bd, 16 * 16)
            nc.vector.tensor_scalar(BD[:, 0:2, :], BD[:, 0:2, :], float(MUL) ** -0.5, None, ALU.mult)
            link(nc.vector.tensor_scalar(BD[:, 2:4, :], BD[:, 2:4, :],
                                         0.5 * float(2 * MUL) ** -0.5 * 16.0 ** -0.5 * float(RN) ** -0.5,
                                         None, ALU.mult))
            link(nc.vector.tensor_scalar(BD[0:MUL, 3, 0:MUL], BD[0:MUL, 3, 0:MUL], 3.0 ** -0.5, None, ALU.mult))
            nc.vector.tensor_copy(BDN[:, :, 0:MUL], BD[:, :, 0:MUL])
            for m in range(3):
                last = nc.vector.tensor_copy(BDN[:, :, MUL:F].rearrange("p k (u m) -> p k u m", m=3)[:, :, :, m],
                                             BD[:, :, MUL * (m + 1):MUL * (m + 2)])
            last.then_inc(s_bdn, 1)
            rgcn(0)
            settle(v)
            with v.Fori(0, PREP_STEPS) as i:
                table_copies(1, R * F, i)
            root_copies(1)
            rgcn(1)
            def update(i):
                v.wait_ge(x_mm, i + 1)
                x4 = X[:, step_blocks(i), :]
                nc.vector.tensor_tensor(x4, x4, PS[:, B_UP, :].rearrange("p (c f) -> p c f", f=F),
                                        ALU.add).then_inc(x_ev, 1)
                v.wait_ge(x_ev, i + 2)
                statistics(1, i)

            for i in range(2):
                update(i)
                scale_and_shift(1, i)
            with v.Fori(0, PREP_STEPS - 2) as i:
                update(i + 2)
                scale_and_shift(1, i + 2)
                table_copies(2, F, i)
            for i in (PREP_STEPS - 2, PREP_STEPS - 1):
                table_copies(2, F, i)
            root_copies(2)
            for h in range(2):
                v.wait_ge(s_zero[h], 1)
            v.wait_ge(ht_ready[2], PREP_STEPS)
            link(nc.vector.memset(PS[:, B_OUT + 1, :], 0.0))
            conv()
            with v.Fori(0, PREP_STEPS) as i:
                v.wait_ge(f_mm, i + 1)
                x4 = X[:, ds(i * PREP, PREP), :]
                nc.vector.tensor_tensor(x4, x4, PS[:, ds(B_TAB + i % 2, 1), :].rearrange("p o (c f) -> p (o c) f", f=F),
                                        ALU.add).then_inc(f_add, 1)

        @block.scalar
        def _(act):
            for n in range(3):
                act.sem_inc(t_ev[n][0], 2)

            def roots(n, i):
                act.wait_ge(s_agg[n], i + 1)
                blocks = step_blocks(i)
                nc.scalar.activation(DEV[:, 1, blocks], DEV[:, 0, blocks], ACT.Sqrt).then_inc(s_dev[n], 1)

            def norms(n, i):
                act.wait_ge(s_stat[n], i + 1)
                act.wait_ge(tp_mm[n], i + 1)
                for c in range(PREP):
                    b = ds(i * PREP + c, 1)
                    last = nc.scalar.activation(RW[:, ds(i % 2, 1), c, :].rearrange("p o f -> p (o f)"),
                                                X[:, b, :].rearrange("p o f -> p (o f)"), ACT.Relu,
                                                scale=RDEV[:, b], bias=SHIFT[:, b])
                last.then_inc(s_norm[n], 1)

            def columns(n, i):
                cols = step_cols(i)
                if n == 1:
                    nc.scalar.activation(ACC[:, 0, cols], ACC[:, 0, cols], ACT.Relu).then_inc(ht_ready[n], 1)
                else:
                    act.wait_ge(tp_mm[n // 2], i + 3)
                    nc.scalar.activation(HC[:, cols] if n else ACC[:, 1, cols], PS[:, B_TR, :],
                                         ACT.Copy).then_inc(ht_ready[n], 1)

            def table_copies(n, width, i):
                for c in (0, 2):
                    act.wait_ge(t_mm[n], i * PREP + c + 1)
                    act.wait_ge(t_free[n], i + 1)
                    nc.scalar.activation(TB[:, ds(i % 2, 1), c, 0:width].rearrange("p o f -> p (o f)"),
                                         PS[:, B_TAB + c, 0:width], ACT.Copy).then_inc(t_ev[n][0], 1)

            def stage(n, slot, tiles):
                field = TYP if n < 2 else SRC
                nc.scalar.activation(STAGE[:, slot, :], V[:, field, tiles], ACT.Copy).then_inc(staged[n], 1)

            def stage_ahead(n, i, s):
                act.wait_ge(msg_done[n], i * BODY + s + 2)
                stage(n, (s + 3) % BODY, ds(i * BODY_TILES + (s + 3) * ST_TILES, ST_TILES))

            def normed_table(n, m, width):
                roots(m, 0)
                norms(m, 0)
                columns(n, 0)
                roots(m, 1)
                norms(m, 1)
                with act.Fori(0, PREP_STEPS - 2) as i:
                    roots(m, i + 2)
                    columns(n, i + 1)
                    norms(m, i + 2)
                    table_copies(n, width, i)
                columns(n, PREP_STEPS - 1)
                for i in (PREP_STEPS - 2, PREP_STEPS - 1):
                    table_copies(n, width, i)

            normed_table(0, 0, R * F)
            nb = bodies(act)

            def first_stages(n):
                if n:
                    act.wait_ge(staged[n - 1], nb * BODY + 3)
                for s in range(3):
                    stage(n, s, slice(s * ST_TILES, (s + 1) * ST_TILES))

            def stages(n):
                with act.Fori(0, nb) as i:
                    for s in range(BODY):
                        stage_ahead(n, i, s)

            act.wait_ge(s_edges, 1)
            first_stages(0)
            stages(0)
            first_stages(1)
            act.wait_ge(add_done[0], nb * BODY + 3)
            columns(1, 0)
            with act.Fori(0, PREP_STEPS - 1) as i:
                columns(1, i + 1)
                table_copies(1, R * F, i)
            table_copies(1, R * F, PREP_STEPS - 1)
            stages(1)
            first_stages(2)
            normed_table(2, 1, F)

            def relu(slot, k):
                act.wait_ge(fc1_done, k + 1)
                nc.scalar.activation(HR[:, slot, :], PS[0:RN, B_HID + slot, :], ACT.Relu,
                                     scale=float(NBAS) ** -0.5).then_inc(relu_done, 1)

            relu(0, 0)
            with act.Fori(0, nb) as i:
                for s in range(BODY):
                    k = i * BODY + s
                    act.wait_ge(fc2_done, k + 2)
                    relu((s + 1) % 2, k + 1)
                    act.wait_ge(prod_done, k + 1)
                    for j in range(ST_TILES):
                        act.wait_ge(gathered[s * ST_TILES + j], (i + nb * 2 + 1) * 16)
                        last = nc.scalar.activation(GS[:, s % 2, j, :], GT[:, s * ST_TILES + j, :], ACT.Copy,
                                                    scale=V[:, SH, ds(i * BODY_TILES + s * ST_TILES + j, 1)])
                    last.then_inc(gs_done, 1)
                    stage_ahead(2, i, s)

        @block.tensor
        def _(pe):
            for n in range(3):
                pe.sem_inc(msg_done[n], 2)
            for n in range(2):
                pe.sem_inc(tp_mm[n], 2)
            pe.sem_inc(fc2_done, 2)

            def cols(b, n=1):
                return slice(b * P, (b + n) * P)

            def transposed_rows(n, i):
                pe.wait_ge(s_norm[n], i + 1)
                if i:
                    pe.wait_ge(ht_ready[2 * n], i)
                for c in range(PREP):
                    last = nc.tensor.transpose(PS[:, B_TR, c * P:(c + 1) * P], RW[:, i % 2, c, :], IDENT[:, :])
                last.then_inc(tp_mm[n], 1)

            def transposed_sums(i):
                pe.wait_ge(x_ev, i + 1)
                for c in range(PREP):
                    last = nc.tensor.transpose(PS[:, B_UP, c * P:(c + 1) * P], ACC[:, 1, cols(i * PREP + c)],
                                               IDENT[:, :])
                last.then_inc(x_mm, 1)

            inputs = [ACC[:, 1, :], ACC[:, 0, :], HC[:, :]]

            def table_products(n, i):
                width = R * F if n < 2 else F
                rhs = WREL[:, n, :] if n < 2 else BD[:, 0, :]
                pe.wait_ge(ht_ready[n], i + 1)
                for c in range(PREP):
                    pe.wait_ge(t_ev[n][c % 2], i * 2 + c // 2 + 1)
                    nc.tensor.matmul(PS[:, B_TAB + c, 0:width], inputs[n][:, cols(i * PREP + c)], rhs,
                                     start=True, stop=True).then_inc(t_mm[n], 1)

            def root_products(n):
                for e in range(2):
                    pe.wait_ge(t_ev[n][e], PREP_STEPS * 2 + 2)
                for i in range(PREP_STEPS):
                    pe.wait_ge(r_ev[n], i + 1)
                    bank = B_TAB + i % 4
                    if n < 2:
                        last = nc.tensor.matmul(PS[:, bank, :], ROOT[:, n, :], inputs[n][:, cols(i * PREP, PREP)],
                                                start=True, stop=True)
                    else:
                        for c in range(PREP):
                            last = nc.tensor.matmul(PS[:, bank, c * P:(c + 1) * P], inputs[n][:, cols(i * PREP + c)],
                                                    BDN[:, 1, :], start=True, stop=True)
                    last.then_inc(r_mm[n], 1)

            def rgcn(n):
                with pe.Fori(0, nb) as i:
                    for s in range(BODY):
                        k = i * BODY + s
                        pe.wait_ge(oh_ready[n], k + 1)
                        pe.wait_ge(add_done[n], k + 2)
                        for j in range(ST_TILES):
                            pe.wait_ge(gathered[s * ST_TILES + j], (i + nb * n + 1) * 16)
                            last = nc.tensor.matmul(PS[:, B_OUT + s % 2, 0:WINDOW], GT[:, s * ST_TILES + j, :],
                                                    OH[:, s % 2, j, :], start=j == 0, stop=j == ST_TILES - 1)
                        last.then_inc(msg_done[n], 1)

            pe.wait_ge(s_const, 2)
            pe.wait_ge(s_w, 8 * 16)
            transposed_rows(0, 0)
            for i in range(PREP_STEPS):
                if i + 1 < PREP_STEPS:
                    transposed_rows(0, i + 1)
                table_products(0, i)
            nb = bodies(pe)
            with pe.If(nb > FAST_BODIES):
                pe.wait_ge(g_const, 1)
                pe.wait_ge(g_lane, 1)
                nc.tensor.matmul(PS[:, B_OUT, 0:NS], ONES, SMALL[:, 0, :], start=True, stop=True).then_inc(g_tot, 1)
                with pe.Fori(0, E_TILES) as t:
                    pe.wait_ge(g_hot, t + 1)
                    nc.tensor.matmul(PS[:, B_OUT, 0:NS], LOWER, SMALL[:, 4, :], start=True, stop=True)
                    nc.tensor.matmul(PS[:, B_OUT, 64:64 + NS], ONES, SMALL[:, 4, :], start=True,
                                     stop=True).then_inc(g_rank, 1)
            root_products(0)
            rgcn(0)
            for i in range(PREP_STEPS):
                table_products(1, i)
            root_products(1)
            rgcn(1)
            pe.wait_ge(add_done[1], nb * BODY + 3)
            pe.wait_ge(s_bdn, 1)
            transposed_sums(0)
            transposed_sums(1)
            transposed_rows(1, 0)
            for i in range(PREP_STEPS):
                if i + 2 < PREP_STEPS:
                    transposed_sums(i + 2)
                if i + 1 < PREP_STEPS:
                    transposed_rows(1, i + 1)
                table_products(2, i)
            root_products(2)

            def fc1(slot, bank, loads):
                pe.wait_ge(ea[slot], loads * 16)
                nc.tensor.matmul(PS[0:RN, B_HID + bank, :], FC1[:, :], EA[:, slot, :],
                                 start=True, stop=True).then_inc(fc1_done, 1)

            def fc2(slot):
                for j in range(ST_TILES):
                    last = nc.tensor.matmul(PS[:, B_W + slot, j * F:(j + 1) * F], HR[:, slot, j * P:(j + 1) * P],
                                            FC2[:, :], start=True, stop=True)
                last.then_inc(fc2_done, 1)

            pe.wait_ge(r_ev[2], PREP_STEPS + 4)
            fc1(0, 0, 1)
            fc1(1, 1, 1)
            pe.wait_ge(relu_done, 1)
            fc2(0)
            with pe.Fori(0, nb) as i:
                for s in range(BODY):
                    k = i * BODY + s
                    pe.wait_ge(relu_done, k + 1)
                    fc1((s + 2) % BODY, s % 2, i + 1 + (s + 2) // BODY)
                    pe.wait_ge(relu_done, k + 2)
                    pe.wait_ge(prod_done, k + 2)
                    fc2((s + 1) % 2)
                    pe.wait_ge(prod_done, k + 3)
                    pe.wait_ge(add_done[2], k + 2)
                    for h in range(2):
                        for j in range(ST_TILES):
                            last = nc.tensor.matmul(PS[:, B_OUT + s % 2, h * WINDOW:(h + 1) * WINDOW],
                                                    MSG[:, s % 2, j, h], OH[:, s % 2, j, :],
                                                    start=j == 0, stop=j == ST_TILES - 1)
                    last.then_inc(msg_done[2], 1)
            pe.wait_ge(add_done[2], nb * BODY + 3)
            for i in range(PREP_STEPS):
                pe.wait_ge(f_add, i + 1)
                for c in range(PREP):
                    for h in range(2):
                        last = nc.tensor.matmul(PS[:, B_TAB + i % 2, c * F:(c + 1) * F],
                                                ACC[:, h, cols(i * PREP + c)], BDN[:, 2 + h, :],
                                                start=h == 0, stop=h == 1)
                last.then_inc(f_mm, 1)


def kernel(**a):
    import concourse.bacc as bacc
    from concourse.bass_utils import run_bass_kernel_spmd

    a = {k: np.asarray(x) for k, x in a.items()}

    def lanes(x, **pad):
        x = np.pad(x, (0, IN_TILES * P - E), **pad)
        return np.ascontiguousarray(x.reshape(IN_TILES, P).T)

    dst = np.pad(a["dst"], (0, IN_TILES * P - E), constant_values=NO_NODE)
    arrays = {
        "x": np.pad(a["x"], ((0, NODES - N), (0, 0))),
        "src": lanes(a["src"]),
        "dst": np.ascontiguousarray(dst.reshape(IN_TILES, P).T),
        "typ": lanes(a["edge_type_4"]),
        "ew": lanes(a["edge_weight"], mode="edge"),
        "sh": np.stack([lanes(a["edge_attr_4"][:, k]) for k in range(4)]),
        "basis": np.ascontiguousarray(np.pad(a["edge_attr_10"], ((0, IN_TILES * P - E), (0, 0))).T),
        "dst_st": dst[:FAST_STS * ST_EDGES].reshape(ST_P, 2, ST_EDGES),
        "W1": a["L0_gnn_W1"], "root1": a["L0_gnn_root1"], "b1": a["L0_gnn_b1"],
        "W2": a["L0_gnn_W2"], "root2": a["L0_gnn_root2"], "b2": a["L0_gnn_b2"],
        "si0": a["L1_gnn_W_si_0e"], "si1": a["L1_gnn_W_si_1o"],
        "l1_0": a["L1_gnn_W_l1_0e"], "l1_1": a["L1_gnn_W_l1_1o"],
        "fc1": a["L1_gnn_W_fc1"], "fc2": a["L1_gnn_W_fc2"],
        "l2_0": a["L1_gnn_W_l2_0e"], "l2_1": a["L1_gnn_W_l2_1o"],
    }
    nc = bacc.Bacc("TRN2", target_bir_lowering=False, num_devices=1)
    d = {n: nc.dram_tensor(f"in_{n}", x.shape, mybir.dt.from_np(x.dtype), kind="ExternalInput").ap()
         for n, x in arrays.items()}
    d["out"] = nc.dram_tensor("out_x", (N, F), mybir.dt.float32, kind="ExternalOutput").ap()
    build(nc, d)
    r = run_bass_kernel_spmd(nc, [{f"in_{n}": x for n, x in arrays.items()}], core_ids=[0])
    return r.results[0]["out_x"]
```

```python
from contextlib import ExitStack

import numpy as np

import concourse.bass as bass
from concourse import mybir

P = 128
N = 6250
E = 100000
F = 128
R = 4
MUL = 32
G4 = 4
NBAS = 10
RN = 100
EPS = 1e-5

ST_TILES = 4
ST_EDGES = ST_TILES * P
BODY = 4
BODY_TILES = BODY * ST_TILES
WINDOW = P
NODE_STS = -(-N // P)
FAST_BODIES = -(-(-(-E // ST_EDGES)) // BODY)
GEN_BODIES = -(-(E // ST_EDGES + 1 + NODE_STS) // BODY)
FAST_STS = FAST_BODIES * BODY
GEN_STS = GEN_BODIES * BODY
AHEAD = 4
IN_TILES = (FAST_STS + AHEAD) * ST_TILES
ALL_STS = GEN_STS + AHEAD
ALL_TILES = ALL_STS * ST_TILES
E_TILES = -(-E // P)
NO_NODE = 8191
FAR = 4.0e6

PREP = 4
NODE_BLOCKS = -(-(NODE_STS * P + WINDOW) // (PREP * P)) * PREP
NODES = NODE_BLOCKS * P
PREP_STEPS = NODE_BLOCKS // PREP
COPIES = (3, 1)
X_FIRST = 3 * PREP

PAIR = 2
PAIR_COLS = PAIR * P
PAIRS = -(-NODE_STS // PAIR)
OUT_STEPS = N // PAIR_COLS
OUT_REST = N - OUT_STEPS * PAIR_COLS
LAG = 26
TAIL = FAST_BODIES - LAG
BODY_LOG = BODY.bit_length() - 1

SRC, DST, TYP, EW, SH = 0, 1, 2, 3, 4
FIELDS = 8
ROW = FIELDS + NBAS
ST_P = FAST_STS // 2

def build(nc, d):
    f32, i32 = mybir.dt.float32, mybir.dt.int32
    ALU, ACT, AX = mybir.AluOpType, mybir.ActivationFunctionType, mybir.AxisListType
    IDX = bass.IndirectOffsetOnAxis
    ds = bass.ds

    table_rel = [nc.dram_tensor(f"table_rel{n}", [rows * R, F], f32).ap()
                 for n, rows in enumerate((NODES, PAIRS * PAIR_COLS))]
    table_y = nc.dram_tensor("table_y", [PAIRS * PAIR_COLS, F], f32).ap()
    basis_t = nc.dram_tensor("basis_t", [NBAS, ALL_TILES * P], f32).ap()
    rows_d = nc.dram_tensor("rows_d", [ALL_TILES * P, ROW], f32).ap()
    w0_d = nc.dram_tensor("w0_d", [1, FAST_STS], f32).ap()
    wide_d = nc.dram_tensor("wide_d", [1, FAST_STS], f32).ap()

    ctx = ExitStack()
    with ctx:
        def sb(name, shape, dt=f32):
            return ctx.enter_context(nc.sbuf_tensor(name, shape, dt))

        def sem(name):
            return ctx.enter_context(nc.semaphore(name))

        X = sb("X", [P, NODE_BLOCKS, F])
        ACC = sb("ACC", [P, 2, NODES])
        BN = sb("BN", [P, NODE_BLOCKS, 6])
        MOM = sb("MOM", [P, 5, NODE_BLOCKS])
        DEV = sb("DEV", [P, 2, NODE_BLOCKS])
        RDEV = sb("RDEV", [P, NODE_BLOCKS])
        SHIFT = sb("SHIFT", [P, NODE_BLOCKS])
        RW = sb("RW", [P, 2, PREP, F])
        SUMS = sb("SUMS", [P, PAIR_COLS])
        H = sb("H", [P, PAIR_COLS])
        HALVES = sb("HALVES", [P, 2, PAIR_COLS])
        TB = sb("TB", [P, 2, PREP, R * F])
        V = sb("V", [P, FIELDS, ALL_TILES])
        W0B = sb("W0B", [P, ALL_STS])
        W0I = sb("W0I", [1, ALL_STS + 4], i32)
        NBR = sb("NBR", [1, 2], i32)
        MINMAX = sb("MINMAX", [P, 4])
        MMALL = sb("MMALL", [P, 4])
        WST = sb("WST", [ST_P, 5, 2])
        LEASTI = sb("LEASTI", [ST_P, 2], i32)
        LEAST = sb("LEAST", [ST_P, 2])
        WIDE = sb("WIDE", [1, FAST_STS + 4])
        WREL = sb("WREL", [F, 2, R * F])
        ROOT = sb("ROOT", [F, 2, F])
        BIAS = sb("BIAS", [F, 2])
        BD = sb("BD", [P, 4, F])
        BDN = sb("BDN", [P, 4, F])
        FC1 = sb("FC1", [NBAS, RN])
        FC2 = sb("FC2", [RN, F])
        IDENT = sb("IDENT", [P, P])
        IOTAI = sb("IOTAI", [P, P], i32)
        IOTA = sb("IOTA", [P, P])
        STAGE = sb("STAGE", [P, BODY, ST_TILES], i32)
        GT = sb("GT", [P, BODY_TILES, F])
        OH = sb("OH", [P, 2, ST_TILES, WINDOW])
        GS = sb("GS", [P, 2, ST_TILES, F])
        MSG = TB[:, :, 0:ST_TILES, 0:2 * F].rearrange("p s v (h f) -> p s v h f", f=F)
        DOT = sb("DOT", [P, ST_TILES, 3, MUL])
        DSUM = sb("DSUM", [P, 2, ST_TILES, MUL])
        WBG = sb("WBG", [P, ST_TILES, MUL])
        EA = sb("EA", [NBAS, BODY, ST_EDGES])
        HR = sb("HR", [RN, 2, ST_EDGES])

        PS = ctx.enter_context(nc.psum_tensor("PS", [P, 8, 512], f32))
        B_OUT, B_HID, B_W = 0, 2, 4
        B_UP, B_TR, B_TAB = 2, 3, 4
        B_ROOT, B_FIN = 6, 6

        NS = NODE_STS
        SOME = 4
        land = ACC[:, 0, 0:ALL_TILES * SOME].rearrange("p (t f) -> p t f", f=SOME)
        at = 0

        def carve(n):
            nonlocal at
            at += n
            return ACC[:, 0, at - n:at]

        FILL_TILES = ALL_TILES // 16
        FILL = carve(ROW * FILL_TILES).rearrange("p (t f) -> p t f", f=ROW)
        BLK, TMPE = carve(E_TILES), carve(E_TILES)
        ONES, LOWER = carve(P), carve(P)
        SMALL = carve(8 * NS).rearrange("p (k n) -> p k n", n=NS)
        assert max(at, ALL_TILES * SOME, 4 * ST_EDGES) <= NODES
        DSTS = ACC[0:ST_P, 0, 0:2 * ST_EDGES].rearrange("p (k e) -> p k e", k=2)
        DSTM = ACC[0:ST_P, 0, 2 * ST_EDGES:4 * ST_EDGES].rearrange("p (k e) -> p k e", k=2)
        BLKI = sb("BLKI", [P, E_TILES], i32)[:, :]
        SLOTI = sb("SLOTI", [P, ALL_STS], i32)[:, :]
        SLOT = sb("SLOT", [P, ALL_STS])[:, :]
        EROW = sb("EROW", [P, ROW])[:, :]
        SMALLI = sb("SMALLI", [P, NS], i32)[:, :]
        POSI = sb("POSI", [P, 1], i32)[:, :]

        s_cstep = sem("const_step")
        s_const = sem("const_ready")
        s_settled = sem("settled")
        s_x = [sem(f"x_loaded{k}") for k in range(2)]
        s_w = sem("weights_loaded")
        s_bdz = sem("blocks_zeroed")
        s_bd = sem("blocks_loaded")
        s_bdn = sem("block_weights_ready")
        s_dst = sem("supertile_dst_loaded")
        s_edge = sem("edges_loaded")
        s_epad = sem("edge_pads_set")
        s_basis = sem("basis_copied")
        s_v = sem("vector_chain")
        s_wst = sem("spans_measured")
        s_wst_out = sem("spans_stored")
        s_wst_in = sem("spans_back")
        s_nb = sem("bodies_known")
        s_mm = sem("lane_range")
        s_mmall = sem("weight_range")
        s_edges = sem("table_rows_ready")
        s_bn = [sem(f"statistics{n}") for n in range(2)]
        s_mom = [sem(f"moments{n}") for n in range(2)]
        s_agg = [sem(f"variances{n}") for n in range(2)]
        s_dev = [sem(f"deviations{n}") for n in range(2)]
        s_rdev = [sem(f"reciprocals{n}") for n in range(2)]
        s_stat = [sem(f"scale_and_shift{n}") for n in range(2)]
        s_norm = [sem(f"rows_normed{n}") for n in range(2)]
        g_v = sem("regroup_chain")
        g_fill = sem("fill_ready")
        g_filled = sem("slots_filled")
        g_lane = sem("lane_counts")
        g_tot = sem("block_totals")
        g_tri = sem("regroup_const_step")
        g_const = sem("regroup_const")
        g_hot = sem("block_onehot")
        g_rank = sem("ranks")
        g_row = sem("edge_row_ready")
        g_basis = sem("edge_basis_in")
        g_scat = sem("edge_rows_scattered")
        g_free = sem("edge_row_free")
        g_land = sem("fields_back")
        g_taken = sem("fields_taken")
        g_bt = sem("basis_back")
        tp_mm = [sem(f"rows_transposed{n}") for n in range(2)]
        ht_ready = [sem(f"columns_ready{n}") for n in range(3)]
        t_mm = [sem(f"table_product{n}") for n in range(3)]
        t_ev = [[sem(f"table_copied{n}_{k}") for k in range(2)] for n in range(3)]
        t_out = [[sem(f"table_stored{n}_{k}") for k in range(2)] for n in range(3)]
        t_free = [sem(f"table_slot_free{n}") for n in range(3)]
        s_sum = sem("sums_taken")
        s_zero = [sem(f"sums_zeroed{h}") for h in range(2)]
        r_mm = [sem(f"root_product{n}") for n in range(3)]
        r_ev = [sem(f"root_copied{n}") for n in range(3)]
        staged = [sem(f"indices_staged{n}") for n in range(3)]
        msg_done = [sem(f"messages_summed{n}") for n in range(3)]
        add_done = [sem(f"sums_added{n}") for n in range(3)]
        oh_ready = [sem(f"onehots_ready{n}") for n in range(2)]
        gathered = [sem(f"gathered{j}") for j in range(BODY_TILES)]
        ea = [sem(f"basis_in{j}") for j in range(BODY)]
        fc1_done = sem("fc1_done")
        relu_done = sem("relu_done")
        fc2_done = sem("fc2_done")
        gs_done = sem("scaled_rows_ready")
        prod_done = sem("products_done")
        d_step = sem("product_steps")
        x_mm = sem("update_transposed")
        x_ev = sem("update_added")
        f_sum = sem("final_sums_taken")
        f_mm = sem("final_product")
        f_add = sem("final_added")
        s_out = sem("result_stored")

        block = ctx.enter_context(nc.Block())


        def step_cols(i):
            return ds(i * PREP * P, PREP * P)

        def pair_cols(b):
            return ds(b * PAIR_COLS, PAIR_COLS)

        def step_blocks(i):
            return ds(i * PREP, PREP)

        def bodies(e):
            e.wait_ge(s_nb, 1)
            return e.value_load(NBR[0:1, 0:1], min_val=FAST_BODIES, max_val=GEN_BODIES)

        def first_after(e):
            return e.value_load(NBR[0:1, 1:2], min_val=0, max_val=TAIL)

        def edge_loop(e, nb, body, stages):
            with e.If(nb > FAST_BODIES):
                with e.Fori(0, nb) as i:
                    at = body(i)
                    for s in range(BODY):
                        at(s)
            with e.If(nb < GEN_BODIES):
                with e.Fori(0, LAG) as i:
                    at = body(i)
                    for s in range(BODY):
                        at(s)
                with e.Fori(LAG, FAST_BODIES) as i:
                    at = body(i)
                    for s in range(BODY):
                        at(s)
                        stages(s, i - LAG, i)


        def settle(e):
            e.sem_inc(s_settled, 1)

        @block.sync
        def _(sp):
            for n in range(3):
                sp.sem_inc(t_free[n], 2)
            x_v = d["x"].rearrange("(b p) f -> p b f", p=P)

            def load_x(k, b):
                sp.dma_start(X[:, b, :], x_v[:, b, :]).then_inc(s_x[k], 16)

            load_x(0, slice(0, X_FIRST))
            for l in range(2):
                sp.dma_start(WREL[:, l, :].rearrange("i (r o) -> i r o", r=R),
                             d[f"W{l + 1}"].rearrange("r i o -> i r o")).then_inc(s_w, 16)
                sp.dma_start(ROOT[:, l, :], d[f"root{l + 1}"]).then_inc(s_w, 16)
                sp.dma_start(BIAS[:, l:l + 1], d[f"b{l + 1}"].rearrange("(f o) -> f o", o=1)).then_inc(s_w, 16)
            sp.dma_start(FC1[:, :], d["fc1"]).then_inc(s_w, 16)
            sp.dma_start(FC2[:, :], d["fc2"]).then_inc(s_w, 16)
            load_x(1, slice(X_FIRST, NODE_BLOCKS))
            sp.wait_ge(s_wst, 1)
            sp.dma_start(w0_d.rearrange("o (p k) -> (o p) k", k=2), WST[:, 0, :]).then_inc(s_wst_out, 16)
            sp.dma_start(wide_d.rearrange("o (p k) -> (o p) k", k=2), WST[:, 3, :]).then_inc(s_wst_out, 16)
            sp.wait_ge(s_wst_out, 32)
            sp.dma_start(WIDE[:, 0:FAST_STS], wide_d).then_inc(s_wst_in, 16)
            sp.dma_start(W0B[:, 0:FAST_STS], w0_d.to_broadcast([P, FAST_STS])).then_inc(s_wst_in, 16)

            def table_out(n, width, dst):
                dst = dst.rearrange("(c p) f -> p c f", p=P)

                def store(i, parity):
                    for e, c in enumerate(COPIES):
                        sp.wait_ge(t_ev[n][e], i * c + 2 * c)
                        settle(sp)
                    sp.dma_start(dst[:, step_blocks(i), :], TB[:, parity, :, 0:width]).then_inc(t_out[n][parity], 16)

                store(0, 0)
                with sp.Fori(0, PREP_STEPS // 2) as j:
                    for q in range(2):
                        store(j * 2 + 1 + q, 1 - q)
                        sp.wait_ge(t_out[n][q], j * 16 + 16)
                        sp.sem_inc(t_free[n], 1)

            relations = [t.rearrange("(n r) f -> n (r f)", r=R) for t in table_rel]
            table_out(0, R * F, relations[0])
            sp.wait_ge(s_bdz, 1)
            for q in range(G4):
                r = slice(MUL * q, MUL * q + MUL)
                k = min(q, 1)
                rx = r if q == 0 else slice(MUL + q - 1, F, 3)
                sp.dma_start(BD[rx, 0, r], d[f"l1_{k}"]).then_inc(s_bd, 16)
                sp.dma_start(BD[rx, 1, r], d[f"si{k}"]).then_inc(s_bd, 16)
                sp.dma_start(BD[r, 2, r], d[f"l2_{k}"][0:MUL, :]).then_inc(s_bd, 16)
                sp.dma_start(BD[r, 3, r], d[f"l2_{k}"][MUL:2 * MUL, :]).then_inc(s_bd, 16)
            sp.dma_start(basis_t[:, 0:IN_TILES * P], d["basis"]).then_inc(s_basis, 16)
            sp.wait_ge(s_basis, 16)
            nb = bodies(sp)

            with sp.If(nb > FAST_BODIES):
                sp.wait_ge(g_fill, 1)
                fill_v = rows_d.rearrange("(c p t) f -> c p t f", c=16, p=P)
                for c in range(16):
                    sp.dma_start(fill_v[c], FILL).then_inc(g_filled, 16)
                with nc.allow_non_contiguous_dma(reason="edges' basis values, one column each"):
                    with sp.Fori(0, E_TILES) as t:
                        sp.wait_ge(g_free, t + 1)
                        sp.dma_start(EROW[:, FIELDS:ROW],
                                     d["basis"][:, ds(t * P, P)].rearrange("k p -> p k")).then_inc(g_basis, 16)
                sp.wait_ge(g_free, E_TILES + 1)
                for k in range(FIELDS // SOME):
                    if k:
                        sp.wait_ge(g_taken, k)
                    sp.dma_start(land, rows_d.rearrange("(t p) f -> p t f", p=P)[:, :, k * SOME:(k + 1) * SOME]
                                 ).then_inc(g_land, 16)
                with nc.allow_non_contiguous_dma(reason="basis values, transposed"):
                    with sp.Fori(0, ALL_STS) as s:
                        sp.dma_start(basis_t[:, ds(s * ST_EDGES, ST_EDGES)],
                                     rows_d[ds(s * ST_EDGES, ST_EDGES), FIELDS:ROW].rearrange("e k -> k e")
                                     ).then_inc(g_bt, 16)
                        sp.wait_ge(g_bt, s * 16 + 16)
                        settle(sp)

            def blocks_out(n, width, dst):
                dst = dst.rearrange("(c p) f -> p c f", p=P)

                def store(b, parity):
                    sp.wait_ge(t_ev[n][0], b + 2)
                    sp.dma_start(dst[:, ds(b * PAIR, PAIR), :], TB[:, parity, 0:PAIR, 0:width]
                                 ).then_inc(t_out[n][parity], 16)

                store(0, 0)
                with sp.Fori(0, PAIRS // 2) as j:
                    for q in range(2):
                        store(j * 2 + 1 + q, 1 - q)
                        sp.wait_ge(t_out[n][q], j * 16 + 16)
                        sp.sem_inc(t_free[n], 1)

            blocks_out(1, R * F, relations[1])
            blocks_out(2, F, table_y)

            for s in range(BODY):
                sp.dma_start(EA[:, s, :], basis_t[:, s * ST_EDGES:(s + 1) * ST_EDGES]).then_inc(ea[s], 16)
            with sp.Fori(0, nb) as i:
                for s in range(BODY):
                    sp.wait_ge(fc1_done, i * BODY + s + 1)
                    sp.dma_start(EA[:, s, :], basis_t[:, ds((i * BODY + BODY + s) * ST_EDGES, ST_EDGES)]
                                 ).then_inc(ea[s], 16)

            def result_out(step, steps):
                rows = d["out"][step * PAIR_COLS:(step + steps) * PAIR_COLS, :]
                sp.wait_ge(f_add, step + steps + 1)
                sp.dma_start(rows.rearrange("(c p) f -> p c f", p=P),
                             X[:, step * PAIR:(step + steps) * PAIR, :]).then_inc(s_out, 16)

            result_out(0, TAIL)
            for step in range(TAIL, OUT_STEPS):
                result_out(step, 1)
            sp.wait_ge(f_add, PAIRS + 1)
            sp.dma_start(d["out"][OUT_STEPS * PAIR_COLS:N, :], X[0:OUT_REST, OUT_STEPS * PAIR, :]).then_inc(s_out, 16)
            sp.wait_ge(s_out, 16 * (OUT_STEPS - TAIL + 2))
            for s in range(BODY):
                sp.wait_ge(ea[s], nb * 16 + 16)
            settle(sp)

        @block.gpsimd
        def _(pool):
            pool.dma_start(DSTS, d["dst_st"]).then_inc(s_dst, 16)
            pool.dma_start(V[:, SRC, 0:IN_TILES], d["src"]).then_inc(s_edge, 16)
            pool.dma_start(V[:, DST, 0:IN_TILES], d["dst"]).then_inc(s_edge, 16)
            pool.dma_start(V[:, TYP, 0:IN_TILES], d["typ"]).then_inc(s_edge, 16)
            pool.dma_start(V[:, EW, 0:IN_TILES], d["ew"]).then_inc(s_edge, 16)
            pool.dma_start(V[:, SH:SH + 4, 0:IN_TILES], d["sh"].rearrange("k p t -> p k t")).then_inc(s_edge, 16)
            nc.gpsimd.memset(V[:, :, IN_TILES:ALL_TILES], 0.0).then_inc(s_epad, 1)
            nc.gpsimd.memset(BD[:, :, :], 0.0).then_inc(s_bdz, 1)
            nc.gpsimd.iota(LEASTI[:, :], [[1, 2]], base=0, channel_multiplier=2).then_inc(s_const, 1)
            nc.gpsimd.iota(IOTAI[:, :], [[1, P]], base=0, channel_multiplier=0).then_inc(s_const, 1)
            nc.gpsimd.memset(IDENT[:, :], 0.0).then_inc(s_cstep, 1)
            pool.wait_ge(s_cstep, 1)
            nc.gpsimd.affine_select(out=IDENT[:, :], in_=IDENT[:, :], compare_op=ALU.not_equal, fill=1.0,
                                    base=0, pattern=[[-1, P]], channel_multiplier=1).then_inc(s_const, 1)
            nc.gpsimd.memset(W0B[:, FAST_STS:ALL_STS], 0.0).then_inc(s_const, 1)
            pool.wait_ge(s_mm, 1)
            nc.gpsimd.partition_all_reduce(MMALL[:, 0:2], MINMAX[:, 0:2], P,
                                           bass.bass_isa.ReduceOp.max).then_inc(s_mmall, 1)
            nb = bodies(pool)

            with pool.If(nb > FAST_BODIES):
                pool.wait_ge(g_lane, 1)
                nc.gpsimd.memset(ONES, 1.0).then_inc(g_tri, 1)
                nc.gpsimd.memset(LOWER, 0.0).then_inc(g_tri, 1)
                nc.gpsimd.iota(SLOTI, [[ST_EDGES, ALL_STS]], base=0, channel_multiplier=0).then_inc(g_tri, 1)
                pool.wait_ge(g_tri, 3)
                nc.gpsimd.affine_select(out=LOWER, in_=LOWER, compare_op=ALU.is_ge, fill=1.0,
                                        base=0, pattern=[[-1, P]], channel_multiplier=1).then_inc(g_const, 1)
                pool.wait_ge(g_filled, 16 * 16)
                pool.sem_inc(g_free, 1)
                with pool.Fori(0, E_TILES) as t:
                    pool.wait_ge(g_row, t + 1)
                    pool.wait_ge(g_basis, t * 16 + 16)
                    settle(pool)
                    pool.indirect_dma_start(out=rows_d, out_offset=IDX(ap=POSI, axis=0),
                                            in_=EROW, in_offset=None,
                                            bounds_check=ALL_TILES * P - 1, oob_is_err=False).then_inc(g_scat, 16)
                    pool.wait_ge(g_scat, t * 16 + 16)
                    pool.sem_inc(g_free, 1)

            def gathers(n, table):
                stores = PREP_STEPS if n == 0 else PAIRS
                for k in range(2):
                    pool.wait_ge(t_out[n][k], (stores + 1 - k) // 2 * 16)
                with pool.Fori(0, nb) as i:
                    for s in range(BODY):
                        pool.wait_ge(staged[n], i * BODY + s + 1)
                        settle(pool)
                        for j in range(ST_TILES):
                            pool.indirect_dma_start(out=GT[:, s * ST_TILES + j, :], out_offset=None, in_=table,
                                                    in_offset=IDX(ap=STAGE[:, s, j:j + 1], axis=0)
                                                    ).then_inc(gathered[s * ST_TILES + j], 16)

            gathers(0, table_rel[0])
            gathers(1, table_rel[1])
            pool.wait_ge(ht_ready[1], PAIRS)
            nc.gpsimd.memset(ACC[:, 0, :], 0.0).then_inc(s_zero[0], 1)
            pool.wait_ge(s_sum, TAIL)
            nc.gpsimd.memset(ACC[:, 1, 0:TAIL * PAIR_COLS], 0.0).then_inc(s_zero[1], 1)
            pool.wait_ge(s_sum, PAIRS)
            nc.gpsimd.memset(ACC[:, 1, TAIL * PAIR_COLS:NODES], 0.0).then_inc(s_zero[1], 1)
            gathers(2, table_y)

        @block.vector
        def _(v):
            count = {}

            def link(ins, s=s_v):
                count[s.name] = count.get(s.name, 0) + 1
                ins.then_inc(s, 1)
                v.wait_ge(s, count[s.name])

            def statistics(n, i, blocks=PREP):
                for c in range(blocks):
                    b = ds(i * blocks + c, 1)
                    last = nc.vector.bn_stats(BN[:, b, :].rearrange("p o k -> p (o k)"),
                                              X[:, b, :].rearrange("p o f -> p (o f)"))
                last.then_inc(s_bn[n], 1)
                v.wait_ge(s_bn[n], i + 1)
                b = ds(i * blocks, blocks)
                even, odd = BN[:, b, 1], BN[:, b, 4]
                nc.vector.tensor_tensor(MOM[:, 1, b], even, odd, ALU.subtract)
                nc.vector.tensor_tensor(MOM[:, 2, b], BN[:, b, 2], BN[:, b, 5], ALU.add).then_inc(s_mom[n], 1)
                nc.vector.tensor_tensor(MOM[:, 0, b], even, odd, ALU.add)
                v.wait_ge(s_mom[n], i * 2 + 1)
                nc.vector.tensor_scalar(MOM[:, 3, b], MOM[:, 2, b], 1.0 / F, EPS, ALU.mult, ALU.add)
                nc.vector.scalar_tensor_tensor(MOM[:, 4, b], MOM[:, 1, b], 0.25, MOM[:, 1, b],
                                               ALU.mult, ALU.mult).then_inc(s_mom[n], 1)
                v.wait_ge(s_mom[n], i * 2 + 2)
                nc.vector.tensor_tensor(DEV[:, 0, b], MOM[:, 4, b], MOM[:, 3, b], ALU.add).then_inc(s_agg[n], 1)

            def scale_and_shift(n, i, blocks=PREP):
                b = ds(i * blocks, blocks)
                v.wait_ge(s_dev[n], i + 1)
                nc.vector.reciprocal(RDEV[:, b], DEV[:, 1, b]).then_inc(s_rdev[n], 1)
                v.wait_ge(s_rdev[n], i + 1)
                nc.vector.scalar_tensor_tensor(SHIFT[:, b], MOM[:, 0, b], -0.5, RDEV[:, b],
                                               ALU.mult, ALU.mult).then_inc(s_stat[n], 1)

            def table_copies(i):
                for c in range(COPIES[0], PREP):
                    v.wait_ge(t_mm[0], i * PREP + c + 1)
                    v.wait_ge(t_free[0], i + 1)
                    nc.vector.tensor_copy(TB[:, ds(i % 2, 1), c, :].rearrange("p o f -> p (o f)"),
                                          PS[:, B_TAB + c, :]).then_inc(t_ev[0][1], 1)

            def root_copies():
                with v.Fori(0, PREP_STEPS) as i:
                    v.wait_ge(r_mm[0], i + 1)
                    nc.vector.tensor_scalar(ACC[:, 0, step_cols(i)],
                                            PS[:, ds(B_TAB + i % 4, 1), :].rearrange("p o n -> p (o n)"),
                                            BIAS[:, 0:1], None, ALU.add).then_inc(r_ev[0], 1)
                v.wait_ge(r_ev[0], PREP_STEPS + 4)

            v.sem_inc(t_ev[0][1], COPIES[1])
            for n in range(3):
                v.sem_inc(add_done[n], 2)
                v.sem_inc(r_ev[n], 1 if n else 4)
            v.sem_inc(x_ev, 1)
            v.sem_inc(prod_done, 2)
            v.sem_inc(f_add, 1)

            v.wait_ge(s_x[0], 16)
            for i in range(3):
                statistics(0, i)
                scale_and_shift(0, i)
            v.wait_ge(s_dst, 16)
            nc.vector.tensor_reduce(WST[:, 0, :], DSTS, AX.X, ALU.min)
            link(nc.vector.scalar_tensor_tensor(DSTM, DSTS, float(N), DSTS, ALU.is_lt, ALU.mult))
            link(nc.vector.reduce_max(WST[:, 1, :], DSTM, AX.X))
            link(nc.vector.tensor_tensor(WST[:, 2, :], WST[:, 1, :], WST[:, 0, :], ALU.subtract))
            v.wait_ge(s_const, 4)
            link(nc.vector.tensor_single_scalar(LEASTI[:, :], LEASTI[:, :], BODY_LOG, ALU.arith_shift_right))
            link(nc.vector.tensor_copy(LEAST[:, :], LEASTI[:, :]))
            link(nc.vector.tensor_scalar(LEAST[:, :], LEAST[:, :], float(1 - LAG), float(PAIR_COLS), ALU.add, ALU.mult))
            nc.vector.tensor_scalar(WST[:, 4, :], WST[:, 2, :], float(WINDOW), None, ALU.is_ge)
            link(nc.vector.tensor_tensor(LEAST[:, :], LEAST[:, :], WST[:, 0, :], ALU.is_gt))
            nc.vector.tensor_tensor(WST[:, 3, :], WST[:, 4, :], LEAST[:, :], ALU.max).then_inc(s_wst, 1)
            link(nc.vector.memset(W0I[:, :], 0))
            v.wait_ge(s_x[1], 16)
            with v.Fori(0, PREP_STEPS - 3) as i:
                statistics(0, i + 3)
                table_copies(i)
                scale_and_shift(0, i + 3)
            for i in (PREP_STEPS - 3, PREP_STEPS - 2):
                table_copies(i)
            v.wait_ge(s_edge, 5 * 16)
            nc.vector.reduce_max(MINMAX[:, 0:1], V[:, EW, 0:E_TILES], AX.X)
            link(nc.vector.tensor_reduce(MINMAX[:, 2:3], V[:, EW, 0:E_TILES], AX.X, ALU.min))
            nc.vector.tensor_scalar(MINMAX[:, 1:2], MINMAX[:, 2:3], -1.0, None, ALU.mult).then_inc(s_mm, 1)
            v.wait_ge(s_wst_in, 32)
            link(nc.vector.reduce_max(WIDE[:, FAST_STS:FAST_STS + 1], WIDE[:, 0:FAST_STS], AX.X))
            flag = WIDE[:, FAST_STS:FAST_STS + 1]
            nc.vector.tensor_scalar(NBR[:, 1:2], flag, -float(TAIL), float(TAIL), ALU.mult, ALU.add)
            nc.vector.tensor_scalar(NBR[:, 0:1], flag, float(GEN_BODIES - FAST_BODIES),
                                    float(FAST_BODIES), ALU.mult, ALU.add).then_inc(s_nb, 1)
            link(nc.vector.tensor_copy(IOTA[:, :], IOTAI[:, :]))
            table_copies(PREP_STEPS - 1)

            nb = bodies(v)
            tail = first_after(v)
            with v.If(nb > FAST_BODIES):
                def glink(ins):
                    link(ins, g_v)

                glink(nc.vector.memset(FILL, 0.0))
                nc.vector.memset(FILL[:, :, DST:DST + 1], float(NO_NODE)).then_inc(g_fill, 1)
                glink(nc.vector.tensor_copy(BLKI, V[:, DST, 0:E_TILES]))
                glink(nc.vector.tensor_single_scalar(BLKI, BLKI, P.bit_length() - 1,
                                                     ALU.arith_shift_right))
                glink(nc.vector.tensor_copy(BLK, BLKI))
                done = count[g_v.name]
                with v.Fori(0, NS) as b:
                    nc.vector.tensor_scalar(TMPE, BLK, IOTA[:, ds(b, 1)], None, ALU.is_equal).then_inc(g_v, 1)
                    v.wait_ge(g_v, b * 2 + done + 1)
                    nc.vector.reduce_sum(SMALL[:, 0, ds(b, 1)], TMPE, AX.X).then_inc(g_v, 1)
                    v.wait_ge(g_v, b * 2 + done + 2)
                count[g_v.name] += 2 * NS
                nc.vector.memset(SMALL[:, 1:3, :], 0.0).then_inc(g_lane, 1)
                v.wait_ge(g_tot, 1)
                glink(nc.vector.tensor_scalar(SMALLI, PS[:, B_OUT, 0:NS], float(ST_EDGES - 1), None, ALU.add))
                shift = ST_EDGES.bit_length() - 1
                glink(nc.vector.tensor_single_scalar(SMALLI, SMALLI, shift, ALU.arith_shift_right))
                glink(nc.vector.tensor_single_scalar(SMALLI, SMALLI, shift, ALU.arith_shift_left))
                glink(nc.vector.tensor_copy(SMALL[:, 1, 1:NS], SMALLI[:, 0:NS - 1]))
                cur, step = 1, 1
                while step < NS:
                    glink(nc.vector.tensor_copy(SMALL[:, 3 - cur, 0:step], SMALL[:, cur, 0:step]))
                    glink(nc.vector.tensor_tensor(SMALL[:, 3 - cur, step:NS], SMALL[:, cur, step:NS],
                                                  SMALL[:, cur, 0:NS - step], ALU.add))
                    cur, step = 3 - cur, step * 2
                NEXT = SMALL[:, 3, :]
                glink(nc.vector.tensor_copy(NEXT, SMALL[:, cur, :]))
                v.wait_ge(g_const, 1)
                glink(nc.vector.tensor_copy(SLOT, SLOTI))
                glink(nc.vector.memset(W0B[:, :], 0.0))
                done = count[g_v.name]
                with v.Fori(1, NS) as b:
                    nc.vector.scalar_tensor_tensor(W0B[:, :], SLOT, SMALL[:, cur, ds(b, 1)], W0B[:, :],
                                                   ALU.is_ge, ALU.add).then_inc(g_v, 1)
                    v.wait_ge(g_v, b + done)
                count[g_v.name] += NS - 1
                glink(nc.vector.tensor_scalar(W0B[:, :], W0B[:, :], float(P), None, ALU.mult))
                HOT, AT, ATHOT, POS = (SMALL[:, k, :] for k in range(4, 8))
                done = count[g_v.name]
                with v.Fori(0, E_TILES) as t:
                    nc.vector.tensor_scalar(HOT, IOTA[:, 0:NS], BLK[:, ds(t, 1)], None,
                                            ALU.is_equal).then_inc(g_hot, 1)
                    v.wait_ge(g_free, t + 1)
                    nc.vector.tensor_scalar(POS[:, 1:2], V[:, DST, ds(t, 1)], float(N), FAR,
                                            ALU.is_ge, ALU.mult)
                    v.wait_ge(g_hot, t + 1)
                    v.wait_ge(g_rank, t + 1)
                    nc.vector.tensor_tensor(AT, PS[:, B_OUT, 0:NS], NEXT, ALU.add).then_inc(g_v, 1)
                    v.wait_ge(g_v, t * 4 + done + 1)
                    nc.vector.tensor_tensor(ATHOT, AT, HOT, ALU.mult).then_inc(g_v, 1)
                    v.wait_ge(g_v, t * 4 + done + 2)
                    nc.vector.reduce_sum(POS[:, 0:1], ATHOT, AX.X).then_inc(g_v, 1)
                    nc.vector.tensor_tensor(NEXT, NEXT, PS[:, B_OUT, 64:64 + NS], ALU.add).then_inc(g_v, 1)
                    v.wait_ge(g_v, t * 4 + done + 4)
                    nc.vector.tensor_copy(EROW[:, 0:FIELDS], V[:, :, ds(t, 1)].rearrange("p f o -> p (f o)"))
                    nc.vector.tensor_tensor(POSI, POS[:, 0:1], POS[:, 1:2], ALU.add).then_inc(g_row, 1)
                count[g_v.name] += 4 * E_TILES
                for k in range(FIELDS // SOME):
                    v.wait_ge(g_land, 16 * k + 16)
                    nc.vector.tensor_copy(V[:, k * SOME:(k + 1) * SOME, :].rearrange("p f t -> p t f"), land
                                          ).then_inc(g_taken, 1)
                v.wait_ge(g_taken, FIELDS // SOME)

            v.wait_ge(s_const, 4)
            nc.vector.scalar_tensor_tensor(V[:, TYP, :], V[:, SRC, :], float(R), V[:, TYP, :],
                                           ALU.mult, ALU.add).then_inc(s_edges, 1)
            dst4 = V[:, DST, :].rearrange("p (s v) -> p s v", v=ST_TILES)
            nc.vector.tensor_tensor(dst4, dst4, W0B[:, :].unsqueeze(2).to_broadcast([P, ALL_STS, ST_TILES]),
                                    ALU.subtract)
            nc.vector.tensor_copy(W0I[:, 1:1 + ALL_STS], W0B[0:1, :])
            v.wait_ge(s_mmall, 1)
            link(nc.vector.tensor_tensor(MMALL[:, 2:3], MMALL[:, 0:1], MMALL[:, 1:2], ALU.add))
            link(nc.vector.tensor_scalar(MMALL[:, 2:3], MMALL[:, 2:3], 1e-8, None, ALU.add))
            link(nc.vector.reciprocal(MMALL[:, 3:4], MMALL[:, 2:3]))
            link(nc.vector.tensor_scalar(V[:, EW, :], V[:, EW, :], MMALL[:, 1:2], MMALL[:, 3:4],
                                         ALU.add, ALU.mult))

            offs = [v.alloc_register(f"window_{s}") for s in range(BODY)]

            def window_at(s):
                return v.snap(offs[s], min_val=0, max_val=NODES - WINDOW)

            def add_sums(n, half, at, bank, k):
                v.wait_ge(msg_done[n], k + 2)
                v.wait_ge(add_done[n], k + 2)
                acc = ACC[:, half, ds(at, WINDOW)] if n < 2 else ACC[:, :, ds(at, WINDOW)]
                cols = WINDOW if n < 2 else 2 * WINDOW
                sums = PS[:, B_OUT + bank, 0:cols]
                if n == 2:
                    sums = sums.rearrange("p (h w) -> p h w", h=2)
                nc.vector.tensor_tensor(acc, acc, sums, ALU.add).then_inc(add_done[n], 1)

            def table_1_stages(s, b, i=None):
                if s == 1:
                    v.wait_ge(r_mm[1], b + 2)
                    nc.vector.tensor_scalar(ACC[:, 1, pair_cols(b)], PS[:, B_ROOT, 0:PAIR_COLS], BIAS[:, 1:2], None,
                                            ALU.add).then_inc(r_ev[1], 1)

            def table_2_stages(s, b, i=None):
                x1 = X[:, ds(b * PAIR, PAIR), :]

                def rows(bank):
                    return PS[:, bank, 0:PAIR_COLS].rearrange("p (c f) -> p c f", f=F)

                if s == 1:
                    v.wait_ge(x_mm, b + 2)
                    nc.vector.tensor_tensor(x1, x1, rows(B_UP), ALU.add).then_inc(x_ev, 1)
                    v.wait_ge(x_ev, b + 2)
                    settle(v)
                    statistics(1, b, PAIR)
                    scale_and_shift(1, b, PAIR)
                if s == 3:
                    v.wait_ge(r_mm[2], b + 1)
                    nc.vector.tensor_tensor(x1, x1, rows(B_ROOT), ALU.add).then_inc(r_ev[2], 1)

            def windows(i):
                v.load(offs, W0I[0:1, ds(i * BODY, BODY)])
                return [window_at(s) for s in range(BODY)]

            def rgcn(n, stages):
                link(nc.vector.memset(PS[:, B_OUT + 1, :], 0.0))

                def body(i):
                    at = windows(i)

                    def supertile(s):
                        k = i * BODY + s
                        v.wait_ge(msg_done[n], k + 1)
                        for j in range(ST_TILES):
                            t = ds(i * BODY_TILES + s * ST_TILES + j, 1)
                            last = nc.vector.tensor_scalar(OH[:, s % 2, j, :], IOTA[:, :], V[:, DST, t],
                                                           V[:, EW, t], ALU.is_equal, ALU.mult)
                        last.then_inc(oh_ready[n], 1)
                        add_sums(n, n, at[s], (s + 1) % 2, k)
                    return supertile

                edge_loop(v, nb, body, stages)
                v.load([offs[0]], W0I[0:1, ds(nb * BODY, 1)])
                add_sums(n, n, window_at(0), 1, nb * BODY)
                with v.Fori(tail, PAIRS) as b:
                    for s in range(BODY):
                        stages(s, b)

            def final_stages(s, b, i=None):
                if s == 3:
                    v.wait_ge(f_mm, b + 2)
                    x2 = X[:, ds(b * PAIR, PAIR), :]
                    nc.vector.tensor_tensor(x2, x2, PS[:, B_FIN, 0:PAIR_COLS].rearrange("p (c f) -> p c f", f=F),
                                            ALU.add).then_inc(f_add, 1)

            def conv():
                def body(i):
                    at = windows(i)

                    def supertile(s):
                        k = i * BODY + s
                        t = ds(i * BODY_TILES + s * ST_TILES, ST_TILES)
                        four = [P, ST_TILES, 3, MUL]
                        g = GT[:, s * ST_TILES:(s + 1) * ST_TILES, :].rearrange("p v (g u) -> p v g u", u=MUL)
                        gs = GS[:, s % 2, :, :].rearrange("p v (g u) -> p v g u", u=MUL)
                        w = PS[:, B_W + s % 2, :].rearrange("p (v g u) -> p v g u", v=ST_TILES, u=MUL)
                        msg = MSG[:, s % 2].rearrange("p v h (g u) -> p v h g u", u=MUL)
                        sh1 = V[:, SH + 1:SH + 4, t].rearrange("p m v -> p v m").unsqueeze(3).to_broadcast(four)
                        v.wait_ge(msg_done[2], k + 1)
                        v.wait_ge(prod_done, k + 2)
                        nc.vector.tensor_tensor(OH[:, s % 2, :, :],
                                                IOTA[:, :].unsqueeze(1).to_broadcast([P, ST_TILES, WINDOW]),
                                                V[:, DST, t].unsqueeze(2).to_broadcast([P, ST_TILES, WINDOW]),
                                                ALU.is_equal)
                        v.wait_ge(gs_done, k + 1)
                        nc.vector.tensor_tensor(DOT[:, :, :, :], g[:, :, 1:4, :], sh1, ALU.mult).then_inc(d_step, 1)
                        v.wait_ge(fc2_done, k + 3)
                        nc.vector.tensor_tensor(WBG[:, :, :], w[:, :, 1, :], g[:, :, 0, :], ALU.mult
                                                ).then_inc(d_step, 1)
                        v.wait_ge(d_step, k * 4 + 1)
                        nc.vector.tensor_tensor(DSUM[:, 0, :, :], DOT[:, :, 0, :], DOT[:, :, 1, :], ALU.add
                                                ).then_inc(d_step, 1)
                        nc.vector.tensor_tensor(msg[:, :, 0, 0, :], w[:, :, 0, :], gs[:, :, 0, :], ALU.mult)
                        v.wait_ge(d_step, k * 4 + 3)
                        nc.vector.tensor_tensor(DSUM[:, 1, :, :], DSUM[:, 0, :, :], DOT[:, :, 2, :], ALU.add
                                                ).then_inc(d_step, 1)
                        nc.vector.tensor_tensor(msg[:, :, 1, 1:4, :], w[:, :, 2, :].unsqueeze(2).to_broadcast(four),
                                                gs[:, :, 1:4, :], ALU.mult)
                        nc.vector.tensor_tensor(msg[:, :, 0, 1:4, :], WBG[:, :, :].unsqueeze(2).to_broadcast(four),
                                                sh1, ALU.mult)
                        v.wait_ge(d_step, k * 4 + 4)
                        nc.vector.tensor_tensor(msg[:, :, 1, 0, :], w[:, :, 3, :], DSUM[:, 1, :, :], ALU.mult
                                                ).then_inc(prod_done, 1)
                        add_sums(2, None, at[s], (s + 1) % 2, k)
                    return supertile

                edge_loop(v, nb, body, final_stages)
                v.load([offs[0]], W0I[0:1, ds(nb * BODY, 1)])
                add_sums(2, None, window_at(0), 1, nb * BODY)
                with v.Fori(tail, PAIRS) as b:
                    for s in range(BODY):
                        final_stages(s, b)

            v.wait_ge(s_w, 8 * 16)
            root_copies()
            v.wait_ge(s_bd, 16 * 16)
            nc.vector.tensor_scalar(BD[:, 0:2, :], BD[:, 0:2, :], float(MUL) ** -0.5, None, ALU.mult)
            link(nc.vector.tensor_scalar(BD[:, 2:4, :], BD[:, 2:4, :],
                                         0.5 * float(2 * MUL) ** -0.5 * 16.0 ** -0.5 * float(RN) ** -0.5,
                                         None, ALU.mult))
            link(nc.vector.tensor_scalar(BD[0:MUL, 3, 0:MUL], BD[0:MUL, 3, 0:MUL], 3.0 ** -0.5, None, ALU.mult))
            nc.vector.tensor_copy(BDN[:, :, 0:MUL], BD[:, :, 0:MUL])
            for m in range(3):
                last = nc.vector.tensor_copy(BDN[:, :, MUL:F].rearrange("p k (u m) -> p k u m", m=3)[:, :, :, m],
                                             BD[:, :, MUL * (m + 1):MUL * (m + 2)])
            last.then_inc(s_bdn, 1)
            rgcn(0, table_1_stages)
            rgcn(1, table_2_stages)
            for h in range(2):
                v.wait_ge(s_zero[h], 1 + h)
            link(nc.vector.memset(PS[:, B_OUT + 1, :], 0.0))
            conv()
        @block.scalar
        def _(act):
            for n in range(3):
                act.sem_inc(t_ev[n][0], 1 if n else COPIES[0])

            def roots(n, i, blocks=PREP):
                act.wait_ge(s_agg[n], i + 1)
                b = ds(i * blocks, blocks)
                nc.scalar.activation(DEV[:, 1, b], DEV[:, 0, b], ACT.Sqrt).then_inc(s_dev[n], 1)

            def norm(b, row):
                return nc.scalar.activation(row, X[:, b, :].rearrange("p o f -> p (o f)"), ACT.Relu,
                                            scale=RDEV[:, b], bias=SHIFT[:, b])

            def norms(i):
                act.wait_ge(s_stat[0], i + 1)
                act.wait_ge(tp_mm[0], i + 1)
                for c in range(PREP):
                    last = norm(ds(i * PREP + c, 1), RW[:, ds(i % 2, 1), c, :].rearrange("p o f -> p (o f)"))
                last.then_inc(s_norm[0], 1)

            def columns(i):
                act.wait_ge(tp_mm[0], i + 3)
                nc.scalar.activation(ACC[:, 1, step_cols(i)], PS[:, B_TR, :], ACT.Copy).then_inc(ht_ready[0], 1)

            def table_copies(i):
                for c in range(COPIES[0]):
                    act.wait_ge(t_mm[0], i * PREP + c + 1)
                    act.wait_ge(t_free[0], i + 1)
                    nc.scalar.activation(TB[:, ds(i % 2, 1), c, :].rearrange("p o f -> p (o f)"),
                                         PS[:, B_TAB + c, :], ACT.Copy).then_inc(t_ev[0][0], 1)

            def table_copy(n, b):
                act.wait_ge(t_mm[n], b + 1)
                act.wait_ge(t_free[n], b + 1)
                slot = ds(b % 2, 1)
                if n == 1:
                    rows, banks = TB[:, slot, 0:PAIR, :], PS[:, B_TAB:B_TAB + PAIR, :]
                else:
                    rows = TB[:, slot, 0:PAIR, 0:F]
                    banks = PS[:, B_TAB, 0:PAIR_COLS].rearrange("p (c f) -> p c f", f=F)
                nc.scalar.activation(rows.rearrange("p o c f -> p (o c) f"), banks, ACT.Copy).then_inc(t_ev[n][0], 1)

            def sums_added(n, i):
                act.wait_ge(add_done[n], (nb if i is None else i) * BODY + 3)

            def table_1_stages(s, b, i=None):
                if s == 0:
                    sums_added(0, i)
                    act.wait_ge(r_mm[1], b + 1)
                    nc.scalar.activation(H[:, :], ACC[:, 0, pair_cols(b)], ACT.Relu).then_inc(ht_ready[1], 1)
                if s == 1:
                    table_copy(1, b)

            def table_2_stages(s, b, i=None):
                if s == 0:
                    sums_added(1, i)
                    act.wait_ge(x_mm, b + 1)
                    nc.scalar.activation(SUMS[:, :], ACC[:, 1, pair_cols(b)], ACT.Copy).then_inc(s_sum, 1)
                if s == 1:
                    roots(1, b, PAIR)
                    act.wait_ge(s_stat[1], b + 1)
                    for c in range(PAIR):
                        last = norm(ds(b * PAIR + c, 1), RW[:, 0, c, :])
                    last.then_inc(s_norm[1], 1)
                if s == 2:
                    act.wait_ge(tp_mm[1], b + 1)
                    nc.scalar.activation(H[:, :], PS[:, B_TR, 0:PAIR_COLS], ACT.Copy).then_inc(ht_ready[2], 1)
                if s == 3:
                    table_copy(2, b)

            def stage(n, slot, tiles):
                field = TYP if n < 2 else SRC
                nc.scalar.activation(STAGE[:, slot, :], V[:, field, tiles], ACT.Copy).then_inc(staged[n], 1)

            def stage_ahead(n, i, s):
                act.wait_ge(msg_done[n], i * BODY + s + 2)
                stage(n, (s + 3) % BODY, ds(i * BODY_TILES + (s + 3) * ST_TILES, ST_TILES))

            for i in range(2):
                roots(0, i)
                norms(i)
            roots(0, 2)
            columns(0)
            with act.Fori(0, PREP_STEPS - 3) as i:
                columns(i + 1)
                norms(i + 2)
                roots(0, i + 3)
                table_copies(i)
            columns(PREP_STEPS - 2)
            norms(PREP_STEPS - 1)
            table_copies(PREP_STEPS - 3)
            columns(PREP_STEPS - 1)
            for i in (PREP_STEPS - 2, PREP_STEPS - 1):
                table_copies(i)
            nb = bodies(act)
            tail = first_after(act)

            def first_stages(n):
                if n:
                    act.wait_ge(staged[n - 1], nb * BODY + 3)
                for s in range(3):
                    stage(n, s, slice(s * ST_TILES, (s + 1) * ST_TILES))

            def rgcn(n, stages):
                def body(i):
                    return lambda s: stage_ahead(n, i, s)

                first_stages(n)
                edge_loop(act, nb, body, stages)
                with act.Fori(tail, PAIRS) as b:
                    for s in range(BODY):
                        stages(s, b)

            act.wait_ge(s_edges, 1)
            rgcn(0, table_1_stages)
            rgcn(1, table_2_stages)
            first_stages(2)

            def relu(slot, k):
                act.wait_ge(fc1_done, k + 1)
                nc.scalar.activation(HR[:, slot, :], PS[0:RN, B_HID + slot, :], ACT.Relu,
                                     scale=float(NBAS) ** -0.5).then_inc(relu_done, 1)

            def final_stages(s, b, i=None):
                if s == 1:
                    sums_added(2, i)
                    act.wait_ge(f_mm, b + 1)
                    nc.scalar.activation(HALVES[:, :, :], ACC[:, :, pair_cols(b)], ACT.Copy).then_inc(f_sum, 1)

            def conv_body(i):
                def supertile(s):
                    k = i * BODY + s
                    act.wait_ge(fc2_done, k + 2)
                    relu((s + 1) % 2, k + 1)
                    act.wait_ge(prod_done, k + 1)
                    for j in range(ST_TILES):
                        act.wait_ge(gathered[s * ST_TILES + j], (i + nb * 2 + 1) * 16)
                        last = nc.scalar.activation(GS[:, s % 2, j, :], GT[:, s * ST_TILES + j, :], ACT.Copy,
                                                    scale=V[:, SH, ds(i * BODY_TILES + s * ST_TILES + j, 1)])
                    last.then_inc(gs_done, 1)
                    stage_ahead(2, i, s)
                return supertile

            relu(0, 0)
            edge_loop(act, nb, conv_body, final_stages)
            with act.Fori(tail, PAIRS) as b:
                for s in range(BODY):
                    final_stages(s, b)

        @block.tensor
        def _(pe):
            for n in range(3):
                pe.sem_inc(msg_done[n], 2)
            pe.sem_inc(tp_mm[0], 2)
            pe.sem_inc(r_mm[1], 1)
            pe.sem_inc(x_mm, 1)
            pe.sem_inc(f_mm, 1)
            pe.sem_inc(fc2_done, 2)

            def cols(b, n=1):
                return slice(b * P, (b + n) * P)

            def transposed_rows(i):
                pe.wait_ge(s_norm[0], i + 1)
                if i:
                    pe.wait_ge(ht_ready[0], i)
                for c in range(PREP):
                    last = nc.tensor.transpose(PS[:, B_TR, c * P:(c + 1) * P], RW[:, i % 2, c, :], IDENT[:, :])
                last.then_inc(tp_mm[0], 1)

            def table_products(i):
                pe.wait_ge(ht_ready[0], i + 1)
                for c in range(PREP):
                    e = c // COPIES[0]
                    pe.wait_ge(t_ev[0][e], i * COPIES[e] + c % COPIES[0] + 1)
                    nc.tensor.matmul(PS[:, B_TAB + c, :], ACC[:, 1, cols(i * PREP + c)], WREL[:, 0, :],
                                     start=True, stop=True).then_inc(t_mm[0], 1)

            def root_products():
                for e, c in enumerate(COPIES):
                    pe.wait_ge(t_ev[0][e], (PREP_STEPS + 1) * c)
                for i in range(PREP_STEPS):
                    pe.wait_ge(r_ev[0], i + 1)
                    nc.tensor.matmul(PS[:, B_TAB + i % 4, :], ROOT[:, 0, :], ACC[:, 1, cols(i * PREP, PREP)],
                                     start=True, stop=True).then_inc(r_mm[0], 1)

            def table_1_stages(s, b, i=None):
                if s == 0:
                    pe.wait_ge(ht_ready[1], b + 1)
                    pe.wait_ge(t_ev[1][0], b + 1)
                    for c in range(PAIR):
                        last = nc.tensor.matmul(PS[:, B_TAB + c, :], H[:, cols(c)], WREL[:, 1, :],
                                                start=True, stop=True)
                    last.then_inc(t_mm[1], 1)
                    pe.wait_ge(r_ev[1], b + 1)
                    nc.tensor.matmul(PS[:, B_ROOT, 0:PAIR_COLS], ROOT[:, 1, :], H[:, :], start=True,
                                     stop=True).then_inc(r_mm[1], 1)

            def table_2_stages(s, b, i=None):
                if s == 0:
                    pe.wait_ge(s_sum, b + 1)
                    pe.wait_ge(x_ev, b + 1)
                    settle(pe)
                    for c in range(PAIR):
                        last = nc.tensor.transpose(PS[:, B_UP, cols(c)], SUMS[:, cols(c)], IDENT[:, :])
                    last.then_inc(x_mm, 1)
                if s == 1:
                    pe.wait_ge(s_norm[1], b + 1)
                    settle(pe)
                    for c in range(PAIR):
                        last = nc.tensor.transpose(PS[:, B_TR, cols(c)], RW[:, 0, c, :], IDENT[:, :])
                    last.then_inc(tp_mm[1], 1)
                if s == 2:
                    pe.wait_ge(ht_ready[2], b + 1)
                    pe.wait_ge(t_ev[2][0], b + 1)
                    for c in range(PAIR):
                        last = nc.tensor.matmul(PS[:, B_TAB, cols(c)], H[:, cols(c)], BD[:, 0, :],
                                                start=True, stop=True)
                    last.then_inc(t_mm[2], 1)
                    pe.wait_ge(r_ev[2], b + 1)
                    for c in range(PAIR):
                        last = nc.tensor.matmul(PS[:, B_ROOT, cols(c)], H[:, cols(c)], BDN[:, 1, :],
                                                start=True, stop=True)
                    last.then_inc(r_mm[2], 1)

            def rgcn(n, stages):
                def body(i):
                    def supertile(s):
                        k = i * BODY + s
                        pe.wait_ge(oh_ready[n], k + 1)
                        pe.wait_ge(add_done[n], k + 2)
                        for j in range(ST_TILES):
                            pe.wait_ge(gathered[s * ST_TILES + j], (i + nb * n + 1) * 16)
                            last = nc.tensor.matmul(PS[:, B_OUT + s % 2, 0:WINDOW], GT[:, s * ST_TILES + j, :],
                                                    OH[:, s % 2, j, :], start=j == 0, stop=j == ST_TILES - 1)
                        last.then_inc(msg_done[n], 1)
                    return supertile

                edge_loop(pe, nb, body, stages)
                with pe.Fori(tail, PAIRS) as b:
                    for s in range(BODY):
                        stages(s, b)

            pe.wait_ge(s_const, 4)
            pe.wait_ge(s_w, 8 * 16)
            transposed_rows(0)
            for i in range(PREP_STEPS):
                if i + 1 < PREP_STEPS:
                    transposed_rows(i + 1)
                table_products(i)
            nb = bodies(pe)
            tail = first_after(pe)
            with pe.If(nb > FAST_BODIES):
                pe.wait_ge(g_const, 1)
                pe.wait_ge(g_lane, 1)
                nc.tensor.matmul(PS[:, B_OUT, 0:NS], ONES, SMALL[:, 0, :], start=True, stop=True).then_inc(g_tot, 1)
                with pe.Fori(0, E_TILES) as t:
                    pe.wait_ge(g_hot, t + 1)
                    nc.tensor.matmul(PS[:, B_OUT, 0:NS], LOWER, SMALL[:, 4, :], start=True, stop=True)
                    nc.tensor.matmul(PS[:, B_OUT, 64:64 + NS], ONES, SMALL[:, 4, :], start=True,
                                     stop=True).then_inc(g_rank, 1)
            root_products()
            pe.wait_ge(r_ev[0], PREP_STEPS + 4)
            rgcn(0, table_1_stages)
            pe.wait_ge(s_bdn, 1)
            rgcn(1, table_2_stages)

            def fc1(slot, bank, loads):
                pe.wait_ge(ea[slot], loads * 16)
                nc.tensor.matmul(PS[0:RN, B_HID + bank, :], FC1[:, :], EA[:, slot, :],
                                 start=True, stop=True).then_inc(fc1_done, 1)

            def fc2(slot):
                for j in range(ST_TILES):
                    last = nc.tensor.matmul(PS[:, B_W + slot, j * F:(j + 1) * F], HR[:, slot, j * P:(j + 1) * P],
                                            FC2[:, :], start=True, stop=True)
                last.then_inc(fc2_done, 1)

            pe.wait_ge(r_ev[2], PAIRS + 1)
            pe.wait_ge(t_ev[2][0], PAIRS + 1)
            def final_stages(s, b, i=None):
                if s == 2:
                    pe.wait_ge(f_sum, b + 1)
                    pe.wait_ge(f_add, b + 1)
                    for c in range(PAIR):
                        for h in range(2):
                            last = nc.tensor.matmul(PS[:, B_FIN, cols(c)], HALVES[:, h, cols(c)], BDN[:, 2 + h, :],
                                                    start=h == 0, stop=h == 1)
                    last.then_inc(f_mm, 1)

            def conv_body(i):
                def supertile(s):
                    k = i * BODY + s
                    pe.wait_ge(relu_done, k + 1)
                    fc1((s + 2) % BODY, s % 2, i + 1 + (s + 2) // BODY)
                    pe.wait_ge(relu_done, k + 2)
                    pe.wait_ge(prod_done, k + 2)
                    fc2((s + 1) % 2)
                    pe.wait_ge(prod_done, k + 3)
                    pe.wait_ge(add_done[2], k + 2)
                    for h in range(2):
                        for j in range(ST_TILES):
                            last = nc.tensor.matmul(PS[:, B_OUT + s % 2, h * WINDOW:(h + 1) * WINDOW],
                                                    MSG[:, s % 2, j, h], OH[:, s % 2, j, :],
                                                    start=j == 0, stop=j == ST_TILES - 1)
                    last.then_inc(msg_done[2], 1)
                return supertile

            fc1(0, 0, 1)
            fc1(1, 1, 1)
            pe.wait_ge(relu_done, 1)
            fc2(0)
            edge_loop(pe, nb, conv_body, final_stages)
            with pe.Fori(tail, PAIRS) as b:
                for s in range(BODY):
                    final_stages(s, b)


def kernel(**a):
    import concourse.bacc as bacc
    from concourse.bass_utils import run_bass_kernel_spmd

    a = {k: np.asarray(x) for k, x in a.items()}

    def lanes(x, **pad):
        x = np.pad(x, (0, IN_TILES * P - E), **pad)
        return np.ascontiguousarray(x.reshape(IN_TILES, P).T)

    dst = np.pad(a["dst"], (0, IN_TILES * P - E), constant_values=NO_NODE)
    arrays = {
        "x": np.pad(a["x"], ((0, NODES - N), (0, 0))),
        "src": lanes(a["src"]),
        "dst": np.ascontiguousarray(dst.reshape(IN_TILES, P).T),
        "typ": lanes(a["edge_type_4"]),
        "ew": lanes(a["edge_weight"], mode="edge"),
        "sh": np.stack([lanes(a["edge_attr_4"][:, k]) for k in range(4)]),
        "basis": np.ascontiguousarray(np.pad(a["edge_attr_10"], ((0, IN_TILES * P - E), (0, 0))).T),
        "dst_st": dst[:FAST_STS * ST_EDGES].reshape(ST_P, 2, ST_EDGES),
        "W1": a["L0_gnn_W1"], "root1": a["L0_gnn_root1"], "b1": a["L0_gnn_b1"],
        "W2": a["L0_gnn_W2"], "root2": a["L0_gnn_root2"], "b2": a["L0_gnn_b2"],
        "si0": a["L1_gnn_W_si_0e"], "si1": a["L1_gnn_W_si_1o"],
        "l1_0": a["L1_gnn_W_l1_0e"], "l1_1": a["L1_gnn_W_l1_1o"],
        "fc1": a["L1_gnn_W_fc1"], "fc2": a["L1_gnn_W_fc2"],
        "l2_0": a["L1_gnn_W_l2_0e"], "l2_1": a["L1_gnn_W_l2_1o"],
    }
    nc = bacc.Bacc("TRN2", target_bir_lowering=False, num_devices=1)
    d = {n: nc.dram_tensor(f"in_{n}", x.shape, mybir.dt.from_np(x.dtype), kind="ExternalInput").ap()
         for n, x in arrays.items()}
    d["out"] = nc.dram_tensor("out_x", (N, F), mybir.dt.float32, kind="ExternalOutput").ap()
    build(nc, d)
    r = run_bass_kernel_spmd(nc, [{f"in_{n}": x for n, x in arrays.items()}], core_ids=[0])
    return r.results[0]["out_x"]
```
